# Optimizing a Trainium2 kernel written in Bass

```python
import numpy as np
import jax
import jax.numpy as jnp

def _softmax(x, axis=-1):
    return jax.nn.softmax(x, axis=axis)

def _gelu(x):
    return jax.nn.gelu(x, approximate=True)

def _silu(x):
    return jax.nn.silu(x)

def _sigmoid(x):
    return jax.nn.sigmoid(x)

def _layernorm(x, axis=-1, eps=1e-05):
    m = jnp.mean(x, axis=axis, keepdims=True)
    v = jnp.var(x, axis=axis, keepdims=True)
    return (x - m) / jnp.sqrt(v + eps)

def _scatter_add(tgt, idx, src, axis=0):
    return tgt.at[idx].add(src)

def _segment_sum(src, seg, n):
    return jax.ops.segment_sum(src, seg, n)
kernel_name = 'mk_gnn_preln_d2_gnn_r8_1de512'

def setup_inputs(seed: int=0):
    np.random.seed(seed)
    _w = jnp.asarray

    def _rec_inputs():
        import jax
        import jax.numpy as jnp
        _gk = jax.random.key(seed)
        x = -0.0005121 + 1.001 * jax.random.normal(jax.random.fold_in(_gk, 1), (6250, 64), jnp.float32)
        src = jax.random.randint(jax.random.fold_in(_gk, 2), (200000,), 0, 6250, jnp.int32)
        dst = jax.random.randint(jax.random.fold_in(_gk, 3), (200000,), 0, 6250, jnp.int32)
        _o = jnp.argsort(dst, stable=True)
        src = src[_o]
        dst = dst[_o]
        edge_type_32 = jax.random.randint(jax.random.fold_in(_gk, 13), (200000,), 0, 32, jnp.int32)
        edge_weight = jax.random.uniform(jax.random.fold_in(_gk, 14), (200000,), jnp.float32, 0.0, 0.999996)
        return (x, src, dst, edge_type_32, edge_weight)
    x, src, dst, edge_type_32, edge_weight = _rec_inputs()

    def _L0_gnn_setup():
        import jax, jax.numpy as jnp
        import numpy as np
        N = 6250
        E = 100000
        IN = 64
        OUT = 64
        R = 32
        B = 4
        key = jax.random.key(seed)
        ks = jax.random.split(key, 8)
        h = jax.random.normal(ks[0], (N, IN), dtype=jnp.float32)
        weight = jax.random.normal(ks[1], (B, IN, OUT), dtype=jnp.float32) * (1.0 / np.sqrt(IN))
        w_comp = jax.random.normal(ks[2], (R, B), dtype=jnp.float32) * (1.0 / np.sqrt(B))
        bias = jax.random.normal(ks[3], (OUT,), dtype=jnp.float32) * 0.02
        src = jax.random.randint(ks[4], (E,), 0, N)
        dst = jax.random.randint(ks[5], (E,), 0, N)
        etype = jax.random.randint(ks[6], (E,), 0, R)
        edge_norm = jax.random.uniform(ks[7], (E,), dtype=jnp.float32)
        return {'h': h, 'weight': weight, 'w_comp': w_comp, 'bias': bias, 'edge_norm': edge_norm, 'src': src, 'dst': dst, 'etype': etype}
    _L0_gnn_all = _L0_gnn_setup()
    _L0_gnn_in = {k: v for k, v in _L0_gnn_all.items() if k in ('weight', 'w_comp', 'bias')}
    del _L0_gnn_all

    def _L1_gnn_setup():
        import jax, jax.numpy as jnp
        import numpy as np
        N_NODES = 6250

        def _sage_conv(x, src, dst, W_l, b_l, W_r):
            msg = x[src]
            agg = jax.ops.segment_sum(msg, dst, num_segments=N_NODES)
            cnt = jax.ops.segment_sum(jnp.ones((src.shape[0],), x.dtype), dst, num_segments=N_NODES)
            mean = agg / jnp.maximum(cnt, 1.0)[:, None]
            return mean @ W_l + b_l + x @ W_r
        key = jax.random.key(seed)
        ks = jax.random.split(key, 8)
        d_in, hid, d_out = (64, 32, 64)
        E = 100000
        x = jax.random.normal(ks[0], (N_NODES, d_in), dtype=jnp.float32)
        edge_index = jax.random.randint(ks[1], (2, E), 0, N_NODES, dtype=jnp.int64)
        s1 = 1.0 / np.sqrt(d_in)
        s2 = 1.0 / np.sqrt(hid)
        W1_l = jax.random.normal(ks[2], (d_in, hid), dtype=jnp.float32) * s1
        W1_r = jax.random.normal(ks[3], (d_in, hid), dtype=jnp.float32) * s1
        b1 = jnp.zeros((hid,), jnp.float32)
        W2_l = jax.random.normal(ks[4], (hid, d_out), dtype=jnp.float32) * s2
        W2_r = jax.random.normal(ks[5], (hid, d_out), dtype=jnp.float32) * s2
        b2 = jnp.zeros((d_out,), jnp.float32)
        return {'x': x, 'edge_index': edge_index, 'W1_l': W1_l, 'b1': b1, 'W1_r': W1_r, 'W2_l': W2_l, 'b2': b2, 'W2_r': W2_r}
    _L1_gnn_all = _L1_gnn_setup()
    _L1_gnn_in = {k: v for k, v in _L1_gnn_all.items() if k in ('W1_l', 'b1', 'W1_r', 'W2_l', 'b2', 'W2_r')}
    del _L1_gnn_all
    return {'x': x, 'src': src, 'dst': dst, 'edge_type_32': edge_type_32, 'edge_weight': edge_weight, 'L0_gnn_weight': _L0_gnn_in['weight'], 'L0_gnn_w_comp': _L0_gnn_in['w_comp'], 'L0_gnn_bias': _L0_gnn_in['bias'], 'L1_gnn_W1_l': _L1_gnn_in['W1_l'], 'L1_gnn_b1': _L1_gnn_in['b1'], 'L1_gnn_W1_r': _L1_gnn_in['W1_r'], 'L1_gnn_W2_l': _L1_gnn_in['W2_l'], 'L1_gnn_b2': _L1_gnn_in['b2'], 'L1_gnn_W2_r': _L1_gnn_in['W2_r']}

def reference(x, src, dst, edge_type_32, edge_weight, L0_gnn_weight, L0_gnn_w_comp, L0_gnn_bias, L1_gnn_W1_l, L1_gnn_b1, L1_gnn_W1_r, L1_gnn_W2_l, L1_gnn_b2, L1_gnn_W2_r):
    import jax
    import jax.numpy as jnp

    def _L0_gnn_ref(h, weight, w_comp, bias, edge_norm, src, dst, etype):
        import jax, jax.numpy as jnp
        import numpy as np
        N = 6250
        E = 100000
        IN = 64
        OUT = 64
        R = 32
        B = 4
        coeff = w_comp[etype]
        h_src = h[src]
        msg_b = jnp.einsum('ei,bio->ebo', h_src, weight)
        msg = jnp.einsum('ebo,eb->eo', msg_b, coeff)
        msg = msg * edge_norm[:, None]
        agg = jax.ops.segment_sum(msg, dst, num_segments=N)
        return jax.nn.relu(agg + bias)

    def _L1_gnn_ref(x, edge_index, W1_l, b1, W1_r, W2_l, b2, W2_r):
        import jax, jax.numpy as jnp
        import numpy as np
        N_NODES = 6250

        def _sage_conv(x, src, dst, W_l, b_l, W_r):
            msg = x[src]
            agg = jax.ops.segment_sum(msg, dst, num_segments=N_NODES)
            cnt = jax.ops.segment_sum(jnp.ones((src.shape[0],), x.dtype), dst, num_segments=N_NODES)
            mean = agg / jnp.maximum(cnt, 1.0)[:, None]
            return mean @ W_l + b_l + x @ W_r
        src, dst = (edge_index[0], edge_index[1])
        h = jax.nn.relu(_sage_conv(x, src, dst, W1_l, b1, W1_r))
        return _sage_conv(h, src, dst, W2_l, b2, W2_r)
    edge_index = jnp.stack([src, dst])
    h = jnp.maximum(_layernorm(x, axis=-1), 0.0)
    x = x + _L0_gnn_ref(h, L0_gnn_weight, L0_gnn_w_comp, L0_gnn_bias, edge_weight, src, dst, edge_type_32)
    h = jnp.maximum(_layernorm(x, axis=-1), 0.0)
    x = x + _L1_gnn_ref(h, edge_index, L1_gnn_W1_l, L1_gnn_b1, L1_gnn_W1_r, L1_gnn_W2_l, L1_gnn_b2, L1_gnn_W2_r)
    return x

_drawn_inputs = setup_inputs


def setup_inputs(seed=0):
    import zlib

    import numpy as np

    out = dict(_drawn_inputs(seed))
    spreads = {'L1_gnn_b1': (0.0, 0.1), 'L1_gnn_b2': (0.0, 0.1)}
    factors = {'L0_gnn_bias': 7.095}
    for name, (base, spread) in spreads.items():
        noise = np.random.default_rng([zlib.crc32(name.encode()), seed]).standard_normal(out[name].shape)
        drawn = base * np.exp(spread * noise) if base else spread * noise
        out[name] = jnp.asarray(drawn.astype(out[name].dtype))
    for name, factor in factors.items():
        out[name] = (out[name] * factor).astype(out[name].dtype)
    return out
```

```python
from contextlib import ExitStack

import concourse.bass as bass
from concourse import mybir


def gnn_kernel(nc, x, src, dst, etype, weight_e, w_basis, w_comp, bias,
               w1_l, b1, w1_r, w2_l, b2, w2_r, out):
    f32, bf16, i32, u32 = mybir.dt.float32, mybir.dt.bfloat16, mybir.dt.int32, mybir.dt.uint32
    ALU, ACT, AX = mybir.AluOpType, mybir.ActivationFunctionType, mybir.AxisListType.X

    P = 128
    N, D = x.shape
    E = src.shape[0]
    NB, NR = w_basis.shape[0], w_comp.shape[0]
    HID = w1_l.shape[1]
    EPS = 1e-5
    TPG = 4
    WIN = 32
    U = 8
    SUB = 128
    BLK = -(-E // (P * SUB))
    FULL_T = E // SUB
    REST = E - FULL_T * SUB
    GROUPS = -(-(-(-E // SUB)) // (TPG * U)) * U
    STEPS = GROUPS // U
    GB = P // TPG
    GALL = BLK * GB
    TALL = BLK * P
    NBLK = -(-N // P)
    NREST = N - (NBLK - 1) * P
    ACCW = NBLK * P + WIN
    XMAX = -(-N // WIN)
    XP = 125
    XN = N // XP
    CG = 14
    CHUNKS = GROUPS // CG
    TAILG = (FULL_T // TPG) % CG
    assert XP * XN == N and CHUNKS * CG == GROUPS and NR * TPG == P and D == 64

    tables = [nc.dram_tensor(f"table{k}", (N, D), f32).ap() for k in range(3)]
    meta_dram = nc.dram_tensor("meta_dram", (2, GALL), i32).ap()

    with ExitStack() as ctx:
        def sb(name, shape, dt):
            return ctx.enter_context(nc.sbuf_tensor(name, shape, dt))

        def sem(name):
            return ctx.enter_context(nc.semaphore(name))

        dst_rows = sb("dst_rows", [P, BLK, SUB], i32)
        src_rows = sb("src_rows", [P, BLK, SUB], i32)
        wgt_rows = sb("wgt_rows", [P, BLK, SUB], f32)
        edge_rows_f = sb("edge_rows_f", [P, 2, BLK, SUB], f32)
        dst_rows_f, src_rows_f = edge_rows_f[:, 0, :, :], edge_rows_f[:, 1, :, :]
        dst_rel = sb("dst_rel", [P, TALL], f32)
        src_cols = sb("src_cols", [P, TALL], f32)
        wgt_cols = sb("wgt_cols", [P, TALL], f32)
        coef = sb("coef", [P, GROUPS * TPG, NB], f32)
        low_high = sb("low_high", [P, 2, 16], f32)
        low_high_t = sb("low_high_t", [BLK, 2, GB], f32)
        meta_t = sb("meta_t", [BLK, 2, GB], i32)
        meta = sb("meta", [1, 2, GALL], i32)
        base_bc = sb("base_bc", [P, GALL], i32)
        shift = sb("shift", [P, XMAX], f32)
        shift_i = sb("shift_i", [P, XMAX], i32)
        types = sb("types", [P, 2, CG * SUB], i32)
        types_hot = sb("types_hot", [P, 2, CG * SUB], bf16)
        rel_i = sb("rel_i", [P, 1], i32)
        rel_of_p = sb("rel_of_p", [P, 1], f32)
        comp_f = sb("comp_f", [P, TPG * NB], f32)
        comp_r = sb("comp_r", [P, TPG * NB], f32)
        comp_parts = sb("comp_parts", [P, 3, TPG * NB], bf16)
        ident = sb("ident", [P, P], f32)
        iota_i = sb("iota_i", [P, WIN], i32)
        iota = sb("iota", [P, WIN], f32)
        idx = sb("idx", [P, U, TPG], i32)
        rows = sb("rows", [P, U, TPG, D], f32)
        hot = sb("hot", [P, 2, TPG, WIN], f32)
        wts = sb("wts", [P, 2, TPG, NB, WIN], f32)
        x_rel = sb("x_rel", [P, TPG], f32)
        x_hot = sb("x_hot", [P, TPG, WIN], f32)
        x_wts = sb("x_wts", [P, TPG, NB, WIN], f32)
        acc = sb("acc", [P, 2, ACCW], f32)
        node_rows_a = sb("node_rows_a", [P, XN, D], f32)
        xa = node_rows_a[0:XP, :, :]
        g_rows = node_rows_a[:, 0:NBLK, :]
        xc = sb("xc", [P, XN, D], f32)
        iota_pads = sb("iota_pads", [P, SUB], f32)
        xb = types[:, :, :].rearrange("p a n -> p (a n)").bitcast(f32)[:, 0:NBLK * D].rearrange(
            "p (b d) -> p b d", d=D)
        centred = edge_rows_f[:, :, :, :].rearrange("p a b e -> p (a b e)")[:, 0:NBLK * D].rearrange(
            "p (b d) -> p b d", d=D)
        stat = sb("stat", [P, 4, XN], f32)
        recip_cnt = sb("recip_cnt", [P, NBLK], f32)
        basis_sb = sb("basis_sb", [P, 2, D], f32)
        w1_sb = sb("w1_sb", [D, 2 * HID], f32)
        w2l_sb = sb("w2l_sb", [D, D], f32)
        w2r_sb = sb("w2r_sb", [HID, D], f32)
        bias_bc = sb("bias_bc", [P, D], f32)
        b1_bc = sb("b1_bc", [P, HID], f32)
        b2_bc = sb("b2_bc", [P, D], f32)

        ps = ctx.enter_context(nc.psum_tensor("ps", [P, 8, 512], f32))

        s_pad = sem("s_pad")
        s_dst = sem("s_dst")
        s_src = sem("s_src")
        s_wgt = sem("s_wgt")
        s_xa = sem("s_xa")
        s_comp = sem("s_comp")
        s_consts = sem("s_consts")
        s_types = [sem(f"s_types{n}") for n in range(2)]
        types_over = sem("types_over")
        s_xb = sem("s_xb")
        s_types_pad = sem("s_types_pad")
        pool_consts = sem("pool_consts")
        dve_step = sem("dve_step")
        rows_cast = sem("rows_cast")
        low_high_ready = sem("low_high_ready")
        low_high_tr = sem("low_high_tr")
        meta_ready = sem("meta_ready")
        meta_stored = sem("meta_stored")
        meta_back = sem("meta_back")
        tr_done = sem("tr_done")
        dst_copied = sem("dst_copied")
        cols_copied = sem("cols_copied")
        comp_ready = sem("comp_ready")
        hot_ready = sem("hot_ready")
        coef_mm = sem("coef_mm")
        coef_done = sem("coef_done")
        var_ready = sem("var_ready")
        std_ready = sem("std_ready")
        table_rows_ready = sem("table_rows_ready")
        table_stored = sem("table_stored")
        idx_ready = sem("idx_ready")
        slots_free = sem("slots_free")
        gathers_begun = sem("gathers_begun")
        gathered = [sem(f"gathered{u}") for u in range(U)]
        onehot_ready = sem("onehot_ready")
        wts_ready = sem("wts_ready")
        mm_done = sem("mm_done")
        psum_free = sem("psum_free")
        x_step = sem("x_step")
        x_wts_ready = sem("x_wts_ready")
        x_mm_done = sem("x_mm_done")
        sums_ready = sem("sums_ready")
        node_mm = sem("node_mm")
        node_in = sem("node_in")
        ps_read = sem("ps_read")
        s_out = sem("s_out")

        block = ctx.enter_context(nc.Block())

        def node_rows(dram, first, last):
            return dram[first * P:last * P, :].rearrange("(b p) d -> p b d", p=P)

        @block.sync
        def _(sp):
            sp.wait_ge(s_pad, 3)
            full = FULL_T // P
            for dram, tile, s in ((dst, dst_rows, s_dst), (src, src_rows, s_src), (weight_e, wgt_rows, s_wgt)):
                sp.dma_start(tile[:, 0:full, :],
                             dram[0:full * P * SUB].rearrange("(b p e) -> p b e", p=P, e=SUB)).then_inc(s, 16)
                left = FULL_T - full * P
                sp.dma_start(tile[0:left, full, :],
                             dram[full * P * SUB:FULL_T * SUB].rearrange("(p e) -> p e", e=SUB)).then_inc(s, 16)
                sp.dma_start(tile[left:left + 1, full, 0:REST],
                             dram[FULL_T * SUB:E].rearrange("(p e) -> p e", p=1)).then_inc(s, 16)
            sp.wait_ge(meta_ready, 1)
            for k in range(2):
                sp.dma_start(meta_dram[k, :].rearrange("(b g) -> b g", g=GB), meta_t[:, k, :]).then_inc(meta_stored, 16)
            sp.wait_ge(meta_stored, 32)
            sp.dma_start(meta[0:1, :, :], meta_dram.rearrange("(p k) g -> p k g", p=1)).then_inc(meta_back, 16)
            sp.dma_start(base_bc[:, :], meta_dram[0:1, :].to_broadcast([P, GALL])).then_inc(meta_back, 16)
            for c in range(CHUNKS):
                if c >= 2:
                    sp.wait_ge(hot_ready, c - 1)
                for t in range(TPG):
                    dst_t = types[t * NR:(t + 1) * NR, c % 2, :].rearrange("p (g e) -> p g e", e=SUB)
                    if c < CHUNKS - 1:
                        lo = c * CG * TPG * SUB
                        rows_t = etype[lo:lo + CG * TPG * SUB].rearrange("(a g t e) -> a t g e", a=1, t=TPG, e=SUB)
                        sp.dma_start(dst_t, rows_t[:, t, :, :].to_broadcast([NR, CG, SUB])).then_inc(s_types[c % 2], 16)
                        continue
                    if t == 0:
                        sp.wait_ge(s_types_pad, 1)
                    lo = c * CG * TPG * SUB
                    rows_t = etype[lo:lo + TAILG * TPG * SUB].rearrange("(a g t e) -> a t g e", a=1, t=TPG, e=SUB)
                    sp.dma_start(dst_t[:, 0:TAILG, :],
                                 rows_t[:, t, :, :].to_broadcast([NR, TAILG, SUB])).then_inc(s_types[c % 2], 16)
                    lo += (TAILG * TPG + t) * SUB
                    n = min(SUB, E - lo)
                    if n > 0:
                        sp.dma_start(dst_t[:, TAILG, 0:n],
                                     etype[lo:lo + n].rearrange("(a e) -> a e", a=1).to_broadcast([NR, n])
                                     ).then_inc(s_types[c % 2], 16)

            sp.wait_ge(types_over, 1)
            sp.dma_start(xb[:, 0:NBLK - 1, :], node_rows(x, 0, NBLK - 1)).then_inc(s_xb, 16)
            sp.dma_start(xb[0:NREST, NBLK - 1, :], x[(NBLK - 1) * P:N, :]).then_inc(s_xb, 16)

        tail_dmas = TPG + sum(E > ((CHUNKS - 1) * CG * TPG + TAILG * TPG + t) * SUB for t in range(TPG))

        @block.gpsimd
        def _(pool):
            pool.iota(iota_i[:, :], [[1, WIN]], base=0, channel_multiplier=0).then_inc(pool_consts, 1)
            pool.iota(rel_i[:, :], [[0, 1]], base=0, channel_multiplier=1).then_inc(pool_consts, 1)
            pool.iota(shift_i[:, :], [[-WIN, XMAX]], base=-WIN, channel_multiplier=0).then_inc(pool_consts, 1)
            pool.memset(ident[:, :], 0.0).then_inc(pool_consts, 1)
            pool.wait_ge(pool_consts, 4)
            pool.affine_select(out=ident[:, :], in_=ident[:, :], compare_op=ALU.not_equal, fill=1.0, base=0,
                               pattern=[[-1, P]], channel_multiplier=1).then_inc(pool_consts, 1)
            for k in range(3):
                pool.wait_ge(table_stored, (16, 48, 80)[k])
                with pool.Fori(0, STEPS) as it:
                    for u in range(U):
                        pool.wait_ge(idx_ready, it * U + (GROUPS * k + u + 1))
                        pool.wait_ge(slots_free, it * U + (GROUPS * k + u + 1))
                        pool.sem_inc(gathers_begun, 1)
                        for t in range(TPG):
                            pool.indirect_dma_start(
                                rows[:, u, t, :], None, tables[k],
                                bass.IndirectOffsetOnAxis(ap=idx[:, u, t:t + 1].bitcast(u32), axis=0),
                            ).then_inc(gathered[u], 16)

        @block.scalar
        def _(act):
            act.dma_start(xa[:, :, :], x.rearrange("(p j) d -> p j d", p=XP)).then_inc(s_xa, 16)
            act.wait_ge(s_pad, 4)
            for t in range(TPG):
                act.dma_start(comp_f[t * NR:(t + 1) * NR, t * NB:(t + 1) * NB], w_comp).then_inc(s_comp, 16)
            for b in range(NB):
                act.dma_start(basis_sb[(b // 2) * D:(b // 2 + 1) * D, b % 2, :], w_basis[b, :, :]).then_inc(s_consts, 16)
            act.dma_start(w1_sb[:, 0:HID], w1_l).then_inc(s_consts, 16)
            act.dma_start(w1_sb[:, HID:2 * HID], w1_r).then_inc(s_consts, 16)
            act.dma_start(w2l_sb[0:HID, :], w2_l).then_inc(s_consts, 16)
            act.dma_start(w2r_sb[:, :], w2_r).then_inc(s_consts, 16)
            for vec, tile, n in ((bias, bias_bc, D), (b1, b1_bc, HID), (b2, b2_bc, D)):
                act.dma_start(tile[:, :], vec.rearrange("(a n) -> a n", a=1).to_broadcast([P, n])).then_inc(s_consts, 16)
            act.wait_ge(var_ready, 1)
            act.activation(stat[0:XP, 3, :], stat[0:XP, 2, :], ACT.Sqrt).then_inc(std_ready, 1)
            act.wait_ge(table_rows_ready, 1)
            act.dma_start(tables[0].rearrange("(p j) d -> p j d", p=XP), xc[0:XP, :, :]).then_inc(table_stored, 16)
            for n in range(4, 12):
                tile = src_cols if n < 8 else wgt_cols
                q, w = (n % 4) * 512, min(512, TALL - (n % 4) * 512)
                act.wait_ge(tr_done, n + 1)
                act.activation(tile[:, q:q + w], ps[:, n % 6, 0:w], ACT.Copy).then_inc(cols_copied, 1)
            act.wait_ge(cols_copied, 8)
            for k in range(3):
                if k:
                    act.wait_ge(table_rows_ready, k + 1)
                    act.dma_start(node_rows(tables[k], 0, NBLK - 1), g_rows[:, 0:NBLK - 1, :]).then_inc(table_stored, 16)
                    act.dma_start(tables[k][(NBLK - 1) * P:N, :], g_rows[0:NREST, NBLK - 1, :]).then_inc(table_stored, 16)
                with act.Fori(0, STEPS) as it:
                    for u in range(U):
                        act.wait_ge(slots_free, it * U + (GROUPS * k + u + 1))
                        act.activation(idx[:, u, :], src_cols[:, bass.ds(it * (U * TPG) + u * TPG, TPG)],
                                       ACT.Copy).then_inc(idx_ready, 1)
                if k == 0:
                    act.wait_ge(var_ready, 2)
                    act.activation(stat[:, 3, 0:NBLK], stat[:, 2, 0:NBLK], ACT.Sqrt).then_inc(std_ready, 1)
            act.wait_ge(table_rows_ready, 4)
            act.dma_start(node_rows(out, 0, NBLK - 1), g_rows[:, 0:NBLK - 1, :]).then_inc(s_out, 16)
            act.dma_start(out[(NBLK - 1) * P:N, :], g_rows[0:NREST, NBLK - 1, :]).then_inc(s_out, 16)
            act.wait_ge(s_out, 32)

        @block.vector
        def _(dve):
            steps = [0]

            def link(ins):
                steps[0] += 1
                ins.then_inc(dve_step, 1)
                dve.wait_ge(dve_step, steps[0])

            dve.memset(dst_rows[:, BLK - 1, :], -1).then_inc(s_pad, 1)
            dve.memset(src_rows[:, BLK - 1, :], 0).then_inc(s_pad, 1)
            dve.memset(wgt_rows[:, BLK - 1, :], 0.0).then_inc(s_pad, 1)
            dve.memset(w2l_sb[:, :], 0.0)
            dve.memset(comp_f[:, :], 0.0).then_inc(s_pad, 1)
            dve.memset(hot[:, :, :, :], 0.0)

            def norm(rows_in, mid, res, p, n, waits):
                st = stat[0:p, :, 0:n]
                link(dve.tensor_reduce(st[:, 0, :], rows_in, axis=AX, op=ALU.add))
                link(dve.tensor_scalar(st[:, 0, :], st[:, 0, :], 1.0 / D, None, ALU.mult))
                mean = st[:, 0, :].unsqueeze(2).to_broadcast([p, n, D])
                link(dve.tensor_tensor(mid, rows_in, mean, ALU.subtract))
                link(dve.tensor_tensor(res, mid, mid, ALU.mult))
                link(dve.tensor_reduce(st[:, 1, :], res, axis=AX, op=ALU.add))
                dve.tensor_scalar(st[:, 2, :], st[:, 1, :], 1.0 / D, EPS, ALU.mult, ALU.add).then_inc(var_ready, 1)
                dve.wait_ge(std_ready, waits)
                link(dve.reciprocal(st[:, 1, :], st[:, 3, :]))
                scale = st[:, 1, :].unsqueeze(2).to_broadcast([p, n, D])
                return dve.scalar_tensor_tensor(out=res, in0=mid, scalar=0.0, in1=scale, op0=ALU.max, op1=ALU.mult)

            dve.wait_ge(s_xa, 16)
            mid = acc[0:XP, 0, 0:XN * D].rearrange("p (j d) -> p j d", d=D)
            link(norm(xa, mid, xc[0:XP, :, :], XP, XN, 1))
            dve.nop().then_inc(table_rows_ready, 1)
            dve.memset(acc[:, :, :], 0.0)

            dve.wait_ge(s_dst, 48)
            link(dve.tensor_copy(dst_rows_f[:, :, :], dst_rows[:, :, :]))
            dve.wait_ge(s_src, 48)
            link(dve.tensor_copy(src_rows_f[:, :, :], src_rows[:, :, :]))
            dve.engine_nop().then_inc(rows_cast, 1)
            link(dve.tensor_reduce(low_high[:, 1, 0:BLK], dst_rows_f[:, :, :], axis=AX, op=ALU.max))
            last = dst_rows_f[:, BLK - 1, :]
            pads = iota_pads[:, :]
            link(dve.tensor_scalar(pads, last, 0.0, 1.0e6, ALU.is_lt, ALU.mult))
            link(dve.tensor_tensor(pads, pads, last, ALU.add))
            dve.tensor_reduce(low_high[:, 0, 0:BLK - 1], dst_rows_f[:, 0:BLK - 1, :], axis=AX, op=ALU.min)
            link(dve.tensor_reduce(low_high[:, 0, BLK - 1:BLK], pads, axis=AX, op=ALU.min))
            dve.engine_nop().then_inc(low_high_ready, 1)
            dve.wait_ge(low_high_tr, 1)
            tr = ps[0:BLK, 6, 0:2 * P].rearrange("b (k g t) -> b k g t", k=2, t=TPG)
            dve.tensor_reduce(low_high_t[:, 0, :], tr[:, 0, :, :], axis=AX, op=ALU.min)
            link(dve.tensor_reduce(low_high_t[:, 1, :], tr[:, 1, :, :], axis=AX, op=ALU.max))
            link(dve.tensor_scalar(low_high_t[:, 0, :], low_high_t[:, 0, :], float(N - 1), None, ALU.min))
            link(dve.tensor_tensor(low_high_t[:, 1, :], low_high_t[:, 1, :], low_high_t[:, 0, :], ALU.subtract))
            link(dve.tensor_scalar(low_high_t[:, 1, :], low_high_t[:, 1, :], 0.0, None, ALU.max))
            link(dve.tensor_copy(meta_t[:, :, :], low_high_t[:, :, :]))
            dve.tensor_single_scalar(meta_t[:, 1, :], meta_t[:, 1, :], WIN.bit_length() - 1,
                                     ALU.logical_shift_right).then_inc(meta_ready, 1)
            dve.wait_ge(pool_consts, 5)
            dve.tensor_copy(iota[:, :], iota_i[:, :])
            dve.tensor_copy(shift[:, :], shift_i[:, :])
            link(dve.tensor_single_scalar(rel_i[:, :], rel_i[:, :], NR - 1, ALU.bitwise_and))
            link(dve.tensor_copy(rel_of_p[:, :], rel_i[:, :]))
            for n in range(4):
                q, w = n * 512, min(512, TALL - n * 512)
                dve.wait_ge(tr_done, n + 1)
                dve.tensor_copy(dst_rel[:, q:q + w], ps[:, n % 6, 0:w]).then_inc(dst_copied, 1)
            dve.wait_ge(dst_copied, 4)
            dve.wait_ge(meta_back, 32)
            by_group = dst_rel[:, :].rearrange("p (g t) -> p g t", t=TPG)
            link(dve.tensor_tensor(by_group, by_group,
                                   base_bc[:, :].unsqueeze(2).to_broadcast([P, GALL, TPG]), ALU.subtract))
            dve.wait_ge(s_comp, 16 * TPG)
            link(dve.tensor_copy(comp_parts[:, 0, :], comp_f[:, :]))
            link(dve.tensor_tensor(comp_r[:, :], comp_f[:, :], comp_parts[:, 0, :], ALU.subtract))
            link(dve.tensor_copy(comp_parts[:, 1, :], comp_r[:, :]))
            link(dve.tensor_tensor(comp_r[:, :], comp_r[:, :], comp_parts[:, 1, :], ALU.subtract))
            dve.tensor_copy(comp_parts[:, 2, :], comp_r[:, :]).then_inc(comp_ready, 1)
            dve.wait_ge(cols_copied, 8)
            for c in range(CHUNKS):
                n = c // 2
                more = 16 * (TPG * n if c < CHUNKS - 1 else TPG * n + tail_dmas - TPG)
                dve.wait_ge(s_types[c % 2], more + 16 * TPG)
                if c >= 2:
                    dve.wait_ge(coef_mm, c - 1)
                dve.tensor_scalar(types_hot[:, c % 2, :], types[:, c % 2, :], rel_of_p[:, 0:1], None,
                                  ALU.is_equal).then_inc(hot_ready, 1)
                if c == CHUNKS - 3:
                    dve.wait_ge(hot_ready, c + 1)
                    dve.memset(types[:, (CHUNKS - 1) % 2, :], -1).then_inc(s_types_pad, 1)
                for d in ([c - 1] if c else []) + ([c] if c == CHUNKS - 1 else []):
                    dve.wait_ge(coef_mm, d + 1)
                    tiles = slice(d * CG * TPG, (d + 1) * CG * TPG)
                    dve.tensor_tensor(coef[:, tiles, :],
                                      ps[:, 6 + d % 2, 0:CG * TPG * NB].rearrange("p (t b) -> p t b", b=NB),
                                      wgt_cols[:, tiles].unsqueeze(2).to_broadcast([P, CG * TPG, NB]),
                                      ALU.mult).then_inc(coef_done, 1)
            dve.wait_ge(coef_done, CHUNKS)
            dve.memset(xb[:, NBLK - 1, :], 0.0).then_inc(types_over, 1)
            dve.nop().then_inc(slots_free, U)

            iota_w = iota[:, :].unsqueeze(1).to_broadcast([P, TPG, WIN])

            def weigh(into, hots, cf):
                return dve.tensor_tensor(into, hots.unsqueeze(2).to_broadcast([P, TPG, NB, WIN]),
                                         cf.unsqueeze(3).to_broadcast([P, TPG, NB, WIN]), ALU.mult)

            x_done = dve.alloc_register("dve_x_done")
            x_steps = dve.alloc_register("dve_x_steps")
            x_base = dve.alloc_register("dve_x_base")
            prev = dve.alloc_register("dve_prev_base")
            dve.reg_mov(x_done, 0)
            dve.reg_mov(x_steps, 0)
            regs = [dve.alloc_register(f"dve_meta{n}") for n in range(2 * U)]

            def aggregate(k):
                parts, nb = (P, 2) if k == 0 else (D, 1)
                dve.reg_mov(prev, 0)
                dve.memset(ps[:, 1, 0:2 * WIN], 0.0).then_inc(psum_free, 1 if k == 0 else 0) if k == 0 else \
                    link(dve.memset(ps[:, 1, 0:2 * WIN], 0.0))

                def add_sums(slot, base, i_expr):
                    into = acc[0:parts, 0:nb, bass.ds(base, WIN)]
                    dve.wait_ge(mm_done, i_expr + (GROUPS * k + 1))
                    dve.wait_ge(psum_free, i_expr + (GROUPS + 1) * k + 1)
                    dve.tensor_tensor(into, into, ps[0:parts, slot, 0:nb * WIN].rearrange("p (b w) -> p b w", w=WIN),
                                      ALU.add).then_inc(psum_free, 1)

                with dve.Fori(0, STEPS) as it:
                    dve.load(regs[0:U], meta[0:1, 0, bass.ds(it * U, U)])
                    dve.load(regs[U:2 * U], meta[0:1, 1, bass.ds(it * U, U)])
                    for u in range(U):
                        i = it * U + u
                        tile0 = it * (U * TPG) + u * TPG
                        extra = dve.snap(regs[U + u], min_val=0, max_val=XMAX - 1)
                        rel = dst_rel[:, bass.ds(tile0, TPG)]
                        cf = coef[:, bass.ds(tile0, TPG), :]
                        dve.tensor_tensor(hot[:, u % 2, :, :], iota_w, rel.unsqueeze(2).to_broadcast([P, TPG, WIN]),
                                          ALU.is_equal).then_inc(onehot_ready if k == 0 else wts_ready, 1)
                        with dve.If(extra > 0):
                            dve.reg_mov(x_base, regs[u])
                            with dve.Fori(0, extra) as j:
                                dve.tensor_scalar(x_rel[:, :], rel, shift[:, bass.ds(j, 1)], None,
                                                  ALU.add).then_inc(x_step, 1)
                                dve.wait_ge(x_step, dve.snap(x_steps) + 1)
                                ins = dve.tensor_tensor(x_hot[:, :, :], iota_w,
                                                        x_rel[:, :].unsqueeze(2).to_broadcast([P, TPG, WIN]),
                                                        ALU.is_equal)
                                if k == 0:
                                    ins.then_inc(x_step, 1)
                                    dve.wait_ge(x_step, dve.snap(x_steps) + 2)
                                    weigh(x_wts[:, :, :, :], x_hot[:, :, :], cf).then_inc(x_wts_ready, 1)
                                else:
                                    ins.then_inc(x_wts_ready, 1)
                                dve.reg_add(x_base, x_base, WIN)
                                into = acc[0:parts, 0:nb,
                                           bass.ds(dve.snap(x_base, min_val=0, max_val=ACCW - WIN), WIN)]
                                dve.wait_ge(x_mm_done, dve.snap(x_done) + 1)
                                dve.wait_ge(psum_free, i + (GROUPS + 1) * k + 1)
                                dve.tensor_tensor(into, into,
                                                  ps[0:parts, 2, 0:nb * WIN].rearrange("p (b w) -> p b w", w=WIN),
                                                  ALU.add).then_inc(x_step, 1)
                                dve.reg_add(x_done, x_done, 1)
                                dve.reg_add(x_steps, x_steps, 3 if k == 0 else 2)
                                dve.wait_ge(x_step, dve.snap(x_steps))
                        if k == 0:
                            dve.wait_ge(onehot_ready, i + 1)
                            weigh(wts[:, u % 2, :, :, :], hot[:, u % 2, :, :], cf).then_inc(wts_ready, 1)
                        add_sums((u + 1) % 2, dve.snap(prev, min_val=0, max_val=N - 1), i)
                        dve.reg_mov(prev, regs[u])
                add_sums(1, dve.snap(prev, min_val=0, max_val=N - 1), GROUPS)
                dve.wait_ge(psum_free, (GROUPS + 1) * (k + 1) + 1)
                dve.nop().then_inc(sums_ready, 1)

            def banks(width, p=P):
                return ps[0:p, 0:-(-NBLK // 8), :].rearrange("p k (b d) -> p (k b) d", d=D)[:, 0:NBLK, 0:width]

            def per_node(v, w):
                return v.unsqueeze(2).to_broadcast([P, NBLK, w])

            def per_feature(v, w):
                return v.unsqueeze(1).to_broadcast([P, NBLK, w])

            def transposed(n, p, into):
                for q in range(-(-NBLK // 4)):
                    w = min(4, NBLK - 4 * q) * P
                    dve.wait_ge(node_mm, n + q + 1)
                    dve.tensor_copy(into[:, q * 512:q * 512 + w], ps[0:p, q % 8, 0:w]).then_inc(ps_read, 1)

            NQ = -(-NBLK // 4)
            xb_v, g_v, xc_v = xb[:, :, :], g_rows, xc[:, 0:NBLK, :]

            aggregate(0)
            dve.wait_ge(s_consts, 16 * (NB + 4 + 3))
            dve.wait_ge(s_xb, 32)
            dve.wait_ge(node_mm, 1)
            link(dve.tensor_tensor(xc_v, banks(D), per_feature(bias_bc[:, :], D), ALU.add))
            link(dve.scalar_tensor_tensor(out=xb_v, in0=xc_v, scalar=0.0, in1=xb_v, op0=ALU.max, op1=ALU.add))
            link(norm(xb_v, centred, xc_v, P, NBLK, 2))
            dve.nop().then_inc(node_in, 1)
            transposed(1, D, acc[0:D, 1, 0:NBLK * P])
            dve.wait_ge(ps_read, NQ)
            dve.memset(acc[0:D, 0, :], 0.0)
            dve.nop().then_inc(node_in, 1)
            dve.wait_ge(node_mm, 2 + NQ)
            link(dve.memset(g_v[:, :, HID:D], 0.0))
            link(dve.memset(g_v[:, :, HID:HID + 1], 1.0))
            link(dve.tensor_copy(g_v[:, :, 0:HID], banks(HID)))
            dve.nop().then_inc(table_rows_ready, 1)
            right1 = xc_v[:, :, 0:HID]
            link(dve.tensor_tensor(right1, banks(2 * HID)[:, :, HID:2 * HID], per_feature(b1_bc[:, :], HID), ALU.add))
            aggregate(1)
            dve.wait_ge(node_mm, 3 + NQ)
            link(dve.tensor_scalar(recip_cnt[:, :].unsqueeze(2), banks(HID + 1)[:, :, HID:HID + 1], 1.0, None, ALU.max))
            link(dve.reciprocal(recip_cnt[:, :], recip_cnt[:, :]))
            hid = g_v[:, :, 0:HID]
            link(dve.tensor_tensor(hid, banks(HID), per_node(recip_cnt[:, :], HID), ALU.mult))
            link(dve.tensor_tensor(hid, hid, right1, ALU.add))
            link(dve.tensor_scalar(hid, hid, 0.0, None, ALU.max))
            dve.nop().then_inc(table_rows_ready, 1)
            dve.nop().then_inc(node_in, 1)
            transposed(3 + NQ, HID, acc[0:HID, 1, 0:NBLK * P])
            dve.wait_ge(ps_read, 2 * NQ)
            dve.memset(acc[0:D, 0, :], 0.0)
            dve.nop().then_inc(node_in, 1)
            dve.wait_ge(node_mm, 4 + 2 * NQ)
            link(dve.tensor_tensor(xb_v, xb_v, banks(D), ALU.add))
            link(dve.tensor_tensor(xb_v, xb_v, per_feature(b2_bc[:, :], D), ALU.add))
            aggregate(2)
            dve.wait_ge(node_mm, 5 + 2 * NQ)
            dve.wait_ge(table_stored, 80)
            link(dve.tensor_tensor(g_v, banks(D), per_node(recip_cnt[:, :], D), ALU.mult))
            link(dve.tensor_tensor(g_v, g_v, xb_v, ALU.add))
            dve.nop().then_inc(table_rows_ready, 1)

        @block.tensor
        def _(pe):
            pe.wait_ge(pool_consts, 5)
            pe.wait_ge(low_high_ready, 1)
            for k in range(2):
                ins = pe.transpose(ps[0:BLK, 6, k * P:(k + 1) * P], low_high[:, k, 0:BLK], ident[:, :])
            ins.then_inc(low_high_tr, 1)
            pe.wait_ge(rows_cast, 1)
            for n in range(12):
                tile = (dst_rows_f, src_rows_f, wgt_rows)[n // 4]
                if n == 8:
                    pe.wait_ge(s_wgt, 48)
                if 6 <= n < 10:
                    pe.wait_ge(dst_copied, n - 5)
                elif n >= 10:
                    pe.wait_ge(cols_copied, n - 9)
                for b in range(4 * (n % 4), min(4 * (n % 4) + 4, BLK)):
                    ins = pe.transpose(ps[:, n % 6, (b % 4) * P:(b % 4 + 1) * P], tile[:, b, :], ident[:, :])
                ins.then_inc(tr_done, 1)
            pe.wait_ge(comp_ready, 1)
            for c in range(CHUNKS):
                pe.wait_ge(hot_ready, c + 1)
                if c >= 2:
                    pe.wait_ge(coef_done, c - 1)
                for g in range(CG):
                    for part in range(3):
                        ins = pe.matmul(ps[:, 6 + c % 2, g * TPG * NB:(g + 1) * TPG * NB],
                                        types_hot[:, c % 2, g * SUB:(g + 1) * SUB], comp_parts[:, part, :],
                                        start=part == 0, stop=part == 2)
                ins.then_inc(coef_mm, 1)

            pe.sem_inc(mm_done, 1)
            x_seen = pe.alloc_register("pe_x_seen")
            pe.reg_mov(x_seen, 0)
            regs = [pe.alloc_register(f"pe_extra{n}") for n in range(U)]

            def products(slot, hots, weights, k, u):
                for t in range(TPG):
                    if k:
                        ins = pe.matmul(ps[0:D, slot, 0:WIN], rows[:, u, t, :], hots[:, t, :],
                                        start=t == 0, stop=t == TPG - 1)
                        continue
                    for half in range(2):
                        ins = pe.matmul(ps[half * D:(half + 1) * D, slot, 0:2 * WIN], rows[:, u, t, :],
                                        weights[:, t, 2 * half:2 * half + 2, :].rearrange("p b w -> p (b w)"),
                                        start=t == 0, stop=t == TPG - 1)
                return ins

            def aggregate(k):
                with pe.Fori(0, STEPS) as it:
                    pe.load(regs, meta[0:1, 1, bass.ds(it * U, U)])
                    for u in range(U):
                        i = it * U + u
                        extra = pe.snap(regs[u], min_val=0, max_val=XMAX - 1)
                        pe.wait_ge(gathered[u], it * (16 * TPG) + 16 * TPG * (STEPS * k + 1))
                        with pe.If(extra > 0):
                            with pe.Fori(0, extra):
                                pe.wait_ge(x_wts_ready, pe.snap(x_seen) + 1)
                                products(2, x_hot[:, :, :], x_wts[:, :, :, :], k, u).then_inc(x_mm_done, 1)
                                pe.reg_add(x_seen, x_seen, 1)
                        pe.wait_ge(wts_ready, i + (GROUPS * k + 1))
                        pe.wait_ge(psum_free, i + ((GROUPS + 1) * k + 1))
                        products(u % 2, hot[:, u % 2, :, :], wts[:, u % 2, :, :, :], k, u).then_inc(mm_done, 1)
                        pe.wait_ge(mm_done, i + (GROUPS * k + 2))
                        pe.sem_inc(slots_free, 1)

            def from_sums(wide, rhs):
                for b in range(NBLK):
                    for h in range(len(rhs)):
                        k_rows = rhs[h].shape[0]
                        ins = pe.matmul(ps[:, b // 8, (b % 8) * D:(b % 8) * D + wide],
                                        acc[0:k_rows, h, b * P:(b + 1) * P], rhs[h],
                                        start=h == 0, stop=h == len(rhs) - 1)
                ins.then_inc(node_mm, 1)

            def transposes(tile, wide, read_before):
                for b in range(NBLK):
                    if b % 4 == 0 and b // 4 >= 8:
                        pe.wait_ge(ps_read, read_before + b // 4 - 7)
                    ins = pe.transpose(ps[0:wide, b // 4 % 8, (b % 4) * P:(b % 4 + 1) * P], tile[:, b, 0:wide],
                                       ident[:, :])
                    if b % 4 == 3 or b == NBLK - 1:
                        ins.then_inc(node_mm, 1)

            def from_transposed(p, rhs):
                for b in range(NBLK):
                    ins = pe.matmul(ps[:, b // 8, (b % 8) * D:(b % 8 + 1) * D], acc[0:p, 1, b * P:(b + 1) * P], rhs,
                                    start=True, stop=True)
                ins.then_inc(node_mm, 1)

            NQ = -(-NBLK // 4)
            pe.wait_ge(meta_back, 32)
            pe.wait_ge(s_consts, 16 * (NB + 4 + 3))
            aggregate(0)
            pe.wait_ge(sums_ready, 1)
            from_sums(D, [basis_sb[:, 0, :], basis_sb[:, 1, :]])
            pe.wait_ge(node_in, 1)
            transposes(xc, D, 0)
            pe.wait_ge(node_in, 2)
            from_transposed(D, w1_sb[:, :])
            aggregate(1)
            pe.wait_ge(sums_ready, 2)
            from_sums(HID + 1, [ident[0:D, 0:HID + 1]])
            pe.wait_ge(node_in, 3)
            transposes(g_rows, HID, NQ)
            pe.wait_ge(node_in, 4)
            from_transposed(HID, w2r_sb[:, :])
            aggregate(2)
            pe.wait_ge(sums_ready, 3)
            from_sums(D, [w2l_sb[:, :]])


_INS = ['x', 'src', 'dst', 'edge_type_32', 'edge_weight', 'L0_gnn_weight', 'L0_gnn_w_comp', 'L0_gnn_bias',
        'L1_gnn_W1_l', 'L1_gnn_b1', 'L1_gnn_W1_r', 'L1_gnn_W2_l', 'L1_gnn_b2', 'L1_gnn_W2_r']


def kernel(**inputs):
    import numpy as _np
    import concourse.bacc as _bacc
    from concourse import mybir as _mybir
    from concourse.bass_utils import run_bass_kernel_spmd as _run

    nc = _bacc.Bacc("TRN2", target_bir_lowering=False, num_devices=1)
    arrays, args = {}, []
    for name in _INS:
        a = _np.ascontiguousarray(inputs[name])
        arrays[f"in_{name}"] = a
        args.append(nc.dram_tensor(f"in_{name}", a.shape, _mybir.dt.from_np(a.dtype), kind="ExternalInput").ap())
    args.append(nc.dram_tensor("out_0", tuple(inputs['x'].shape), _mybir.dt.float32, kind="ExternalOutput").ap())
    gnn_kernel(nc, *args)
    r = _run(nc, [arrays], core_ids=[0])
    return r.results[0]["out_0"]
```

```python
from contextlib import ExitStack

import concourse.bass as bass
from concourse import mybir


def gnn_kernel(nc, x, src, dst, etype, weight_e, w_basis, w_comp, bias,
               w1_l, b1, w1_r, w2_l, b2, w2_r, out):
    f32, bf16, i32, u32 = mybir.dt.float32, mybir.dt.bfloat16, mybir.dt.int32, mybir.dt.uint32
    f16, f8 = mybir.dt.float16, mybir.dt.float8e4
    ALU, ACT, AX = mybir.AluOpType, mybir.ActivationFunctionType, mybir.AxisListType.X

    P = 128
    N, D = x.shape
    E = src.shape[0]
    NB, NR = w_basis.shape[0], w_comp.shape[0]
    HID = w1_l.shape[1]
    EPS = 1e-5
    TPG = 4
    WIN = 24
    U = 8
    SUB = 128
    BLK = -(-E // (P * SUB))
    FULL_T = E // SUB
    REST = E - FULL_T * SUB
    GROUPS = -(-(-(-E // SUB)) // (TPG * U)) * U
    STEPS = GROUPS // U
    GB = P // TPG
    GALL = BLK * GB
    TALL = BLK * P
    NBLK = -(-N // P)
    NREST = N - (NBLK - 1) * P
    ACCW = NBLK * P + WIN
    XMAX = -(-N // WIN)
    XP = 125
    XN = N // XP
    ST = U * TPG
    PAD = 1_000_000
    WD = 8
    WCOL = WD * NBLK
    WVIS = 3
    WPS = 2 * U
    NW = WPS * STEPS
    WP, WC = 112, NW // 112
    HW = WPS // 2
    HDST = HW * WD
    HALVES = 2 * STEPS
    EXACT = 16
    CH = 8
    FULLC = HALVES // CH
    RESTH = HALVES - FULLC * CH
    NBUF = 3
    TRIPS = FULLC // NBUF
    H3W = 3 * HID + 1
    TROW = D
    assert XP * XN == N and NR * TPG == P and D == 64 and WP * WC == NW and NW * WD == NBLK * P
    assert CH * HDST == 512 and TRIPS * NBUF == FULLC and RESTH > 0

    tables = [nc.dram_tensor(f"table{k}", (N, D), f32).ap() for k in range(3)]
    meta_dram = nc.dram_tensor("meta_dram", (2, GALL), i32).ap()
    tiles_dram = nc.dram_tensor("tiles_dram", (2, TALL), f32).ap()
    keys_dram = nc.dram_tensor("keys_dram", (TALL, SUB * 2), f32).ap()
    start_dram = nc.dram_tensor("start_dram", (NW,), i32).ap()
    types_dram = nc.dram_tensor("types_dram", ((STEPS + 2) * ST * SUB,), i32).ap()
    a_dram = nc.dram_tensor("a_dram", (HALVES + 3, P, NBLK * HDST // 2), bf16).ap()

    with ExitStack() as ctx:
        def sb(name, shape, dt):
            return ctx.enter_context(nc.sbuf_tensor(name, shape, dt))

        def sem(name):
            return ctx.enter_context(nc.semaphore(name))

        a_words = CH * NBLK * HDST // 4
        arena_rows = sb("arena_rows", [P, a_words], f32)

        def in_arena(arena, n, dt):
            return arena[:, n * TALL:(n + 1) * TALL].bitcast(dt)

        dst_rows, src_rows, wgt_rows = (in_arena(arena_rows, n, dt).rearrange("p (b e) -> p b e", e=SUB)
                                        for n, dt in enumerate((i32, i32, f32)))
        edge_rows_f = sb("edge_rows_f", [P, 2, BLK, SUB], f32)
        dst_rows_f, src_rows_f = edge_rows_f[:, 0, :, :], edge_rows_f[:, 1, :, :]
        arena_cols = sb("arena_cols", [P, a_words], f32)
        dst_rel, src_cols, wgt_cols = (in_arena(arena_cols, n, f32) for n in range(3))
        arena_coef = sb("arena_coef", [P, (STEPS + 1) * ST * NB], f32)
        coef = arena_coef[:, :].rearrange("p (t b) -> p t b", b=NB)
        low_high = sb("low_high", [P, 3, 16], f32)
        low_high_t = sb("low_high_t", [BLK, 2, GB], f32)
        meta_t = sb("meta_t", [BLK, 2, GB], i32)
        tables_i = sb("tables_i", [33, 2 * GALL], i32)
        meta = tables_i[0:1, :].rearrange("p (k g) -> p k g", k=2)
        starts = tables_i[32:33, 0:NW]
        shift = sb("shift", [P, XMAX], f32)
        types = sb("types", [P, U * SUB], i32)
        types_hot = sb("types_hot", [P, U * SUB], bf16)
        no_type = sb("no_type", [64, ((STEPS + 2) * ST * SUB - E) // 64], i32)
        thr_i = sb("thr_i", [P, WC], i32)
        thr = sb("thr", [P, 2, WC], f32)
        tile_cnt = sb("tile_cnt", [P, WC], f32)
        tile_cnt_i = sb("tile_cnt_i", [P, WC], i32)
        edge_cnt = sb("edge_cnt", [P, WC], f32)
        start_i = sb("start_i", [P, WC], i32)
        arena_win = sb("arena_win", [P, NBLK * D], f32)
        win_used = [0]

        def in_arena_win(n, dt):
            win_used[0] += n
            return arena_win[:, win_used[0] - n:win_used[0]].bitcast(dt)

        wbase = in_arena_win(NW, f32)
        iota_l = sb("iota_l", [P, P], f16)
        iota_q = sb("iota_q", [P, WCOL], f16)
        keys = sb("keys", [P, WPS, WVIS, 2], f32)
        key_rel = sb("key_rel", [P, 2, 2, WVIS], f32)
        row_hot = in_arena_win(WVIS * P, bf16).rearrange("p (j v c) -> p j v c", j=2, v=WVIS)
        col_hot = in_arena_win(WVIS * WCOL, bf16).rearrange("p (j v c) -> p j v c", j=2, v=WVIS)
        above = in_arena_win(WCOL // 2, bf16)
        a_half = edge_rows_f[:, :, :, :].rearrange("p a b e -> p (a b e)")[:, 0:NBLK * HDST // 2].bitcast(f8).rearrange(
            "p (h b d) -> p h b d", h=2, b=NBLK)
        above_sum = sb("above_sum", [P, NW], f32)
        base_bc = above_sum[:, 0:GALL].bitcast(i32)
        neg_exact = sb("neg_exact", [P, 1], f32)
        faults = sb("faults", [P, 8], f32)
        fault_i = sb("fault_i", [1, 1], i32)
        ones = sb("ones", [P, 1], f32)
        from_parts = sb("from_parts", [H3W, HID + 1], f32)
        rel_i = sb("rel_i", [P, 1], i32)
        rel_of_p = sb("rel_of_p", [P, 1], f32)
        comp_f = sb("comp_f", [P, TPG * NB], f32)
        comp_r = sb("comp_r", [P, TPG * NB], f32)
        comp_parts = sb("comp_parts", [P, 3, TPG * NB], bf16)
        ident = sb("ident", [P, P], f32)
        iota_i = sb("iota_i", [P, WIN], i32)
        iota = sb("iota", [P, WIN], f32)
        idx = sb("idx", [P, U, TPG], i32)
        rows = sb("rows", [P, U, TPG, D], f32)
        hot = sb("hot", [P, 2, TPG, WIN], f32)
        wts = sb("wts", [P, 2, TPG, NB, WIN], f32)
        x_rel = sb("x_rel", [P, TPG], f32)
        x_hot = sb("x_hot", [P, TPG, WIN], f32)
        x_wts = sb("x_wts", [P, TPG, NB, WIN], f32)
        acc = sb("acc", [P, 2, ACCW], f32)
        keys_all = acc[:, 1, 0:2 * TALL].rearrange("p (b e k) -> p b e k", e=SUB, k=2)
        tile_high = acc[:, 1, 2 * TALL:3 * TALL]
        scratch = acc[:, 0, 0:TALL]
        scratch_i = acc[:, 0, TALL:2 * TALL].bitcast(i32)
        shift_i = acc[:, 0, 4096 + WC * SUB * 2:4096 + WC * SUB * 2 + XMAX].bitcast(i32)
        wbase_i = acc[:, 1, 3 * TALL:3 * TALL + NW].bitcast(i32)
        iota_w_i = acc[:, 1, 3 * TALL + NW:3 * TALL + NW + WCOL].bitcast(i32)
        tiles_t = rows[0:BLK, 0, :, :].rearrange("p t d -> p (t d)")[:, 0:2 * P].rearrange("p (k t) -> p k t", k=2)
        parts3 = acc[:, 1, 0:(NBLK * H3W + 1) // 2].bitcast(bf16)[:, 0:NBLK * H3W].rearrange(
            "p (b c) -> p b c", c=H3W)
        key_rows = acc[0:WP, 0, 4096:4096 + WC * SUB * 2].rearrange("p (c f) -> p c f", f=SUB * 2)
        node_rows_a = sb("node_rows_a", [P, XN, D], f32)
        xa = node_rows_a[0:XP, :, :]
        g_rows = node_rows_a[:, 0:NBLK, :]
        NT = FULL_T + 1
        tile_rows = node_rows_a[0:1, :, :].rearrange("p j d -> p (j d)")[:, 0:2 * NT].rearrange(
            "p (k t) -> p k t", k=2)
        xc = sb("xc", [P, XN, D], f32)
        xb = arena_win[:, :].rearrange("p (b d) -> p b d", d=D)
        centred = edge_rows_f[:, :, :, :].rearrange("p a b e -> p (a b e)")[:, 0:NBLK * D].rearrange(
            "p (b d) -> p b d", d=D)
        stat = sb("stat", [P, 4, XN], f32)
        recip_cnt = sb("recip_cnt", [P, NBLK], f32)
        basis_sb = sb("basis_sb", [P, 2, D], f32)
        w1_sb = sb("w1_sb", [D, 2 * HID], f32)
        w2l_sb = sb("w2l_sb", [H3W, D], f32)
        w2r_sb = sb("w2r_sb", [HID, D], f32)
        bias_bc = sb("bias_bc", [P, D], f32)
        b1_bc = sb("b1_bc", [P, HID], f32)
        b2_bc = sb("b2_bc", [P, D], f32)

        ps = ctx.enter_context(nc.psum_tensor("ps", [P, 8, 512], f32))

        s_pad = sem("s_pad")
        s_dst = sem("s_dst")
        s_src = sem("s_src")
        s_wgt = sem("s_wgt")
        s_xa = sem("s_xa")
        s_comp = sem("s_comp")
        s_consts = sem("s_consts")
        types_stored = sem("types_stored")
        types_loaded = sem("types_loaded")
        pool_consts = sem("pool_consts")
        dve_step = sem("dve_step")
        from_parts_step = sem("from_parts_step")
        rows_cast = sem("rows_cast")
        keys_ready = sem("keys_ready")
        keys_stored = sem("keys_stored")
        low_high_ready = sem("low_high_ready")
        low_high_tr = sem("low_high_tr")
        tiles_ready = sem("tiles_ready")
        tiles_stored = sem("tiles_stored")
        tile_high_back = sem("tile_high_back")
        tile_rows_back = sem("tile_rows_back")
        meta_ready = sem("meta_ready")
        meta_stored = sem("meta_stored")
        meta_back = sem("meta_back")
        tile_cnt_ready = sem("tile_cnt_ready")
        key_rows_in = sem("key_rows_in")
        starts_ready = sem("starts_ready")
        starts_stored = sem("starts_stored")
        starts_back = sem("starts_back")
        tr_done = sem("tr_done")
        dst_copied = sem("dst_copied")
        cols_copied = sem("cols_copied")
        comp_ready = sem("comp_ready")
        types_hot_ready = sem("types_hot_ready")
        coef_mm = sem("coef_mm")
        coef_done = sem("coef_done")
        var_ready = sem("var_ready")
        std_ready = sem("std_ready")
        table_rows_ready = sem("table_rows_ready")
        table_stored = sem("table_stored")
        idx_ready = sem("idx_ready")
        idx_ready_sage = sem("idx_ready_sage")
        gathers_begun = sem("gathers_begun")
        gathered = [sem(f"gathered{u}") for u in range(U)]
        onehot_ready = sem("onehot_ready")
        wts_ready = sem("wts_ready")
        mm_done = sem("mm_done")
        psum_free = sem("psum_free")
        stand_in = sem("stand_in")
        x_step = sem("x_step")
        x_wts_ready = sem("x_wts_ready")
        x_mm_done = sem("x_mm_done")
        extras_begun = sem("extras_begun")
        sums_ready = sem("sums_ready")
        keys_loaded = [sem(f"keys_loaded{n}") for n in range(WPS)]
        key_rel_ready = sem("key_rel_ready")
        hots_ready = sem("hots_ready")
        win_mm = sem("win_mm")
        win_read = sem("win_read")
        copies_begun = sem("copies_begun")
        dense_begun = sem("dense_begun")
        a_stored = [sem(f"a_stored{h}") for h in range(2)]
        windows_over = sem("windows_over")
        s_xb = sem("s_xb")
        faults_mm = sem("faults_mm")
        faults_in = sem("faults_in")
        fault_known = sem("fault_known")
        a_loaded = [sem(f"a_loaded{b}") for b in range(NBUF)]
        parts_ready = sem("parts_ready")
        conv_mm = sem("conv_mm")
        conv_read = sem("conv_read")
        node_mm = sem("node_mm")
        node_in = sem("node_in")
        ps_read = sem("ps_read")
        s_out = sem("s_out")

        block = ctx.enter_context(nc.Block())

        def node_rows(dram, first, last):
            return dram[first * P:last * P, :].rearrange("(b p) d -> p b d", p=P)

        a_buf = [arena[:, 0:a_words].bitcast(f8).rearrange("p (h n) -> p h n", h=CH)
                 for arena in (arena_coef, arena_rows, arena_cols)]
        POOL_CONSTS = 14
        CONST_DMAS = 16 * (NB + 6 + 3)

        @block.sync
        def _(sp):
            sp.wait_ge(s_pad, 3)
            full = FULL_T // P
            for dram, tile, s in ((dst, dst_rows, s_dst), (src, src_rows, s_src), (weight_e, wgt_rows, s_wgt)):
                sp.dma_start(tile[:, 0:full, :],
                             dram[0:full * P * SUB].rearrange("(b p e) -> p b e", p=P, e=SUB)).then_inc(s, 16)
                left = FULL_T - full * P
                sp.dma_start(tile[0:left, full, :],
                             dram[full * P * SUB:FULL_T * SUB].rearrange("(p e) -> p e", e=SUB)).then_inc(s, 16)
                sp.dma_start(tile[left:left + 1, full, 0:REST],
                             dram[FULL_T * SUB:E].rearrange("(p e) -> p e", p=1)).then_inc(s, 16)
            sp.dma_start(types_dram[0:E].rearrange("(a b) -> a b", a=16),
                         etype.rearrange("(a b) -> a b", a=16)).then_inc(types_stored, 16)
            sp.wait_ge(pool_consts, POOL_CONSTS)
            sp.dma_start(types_dram[E:(STEPS + 2) * ST * SUB].rearrange("(a b) -> a b", a=64),
                         no_type[:, :]).then_inc(types_stored, 16)
            def load_types(first_tile):
                rows_t = types_dram[bass.ds(first_tile * SUB, ST * SUB)].rearrange(
                    "(a g t e) -> a t g e", a=1, t=TPG, e=SUB)
                for t in range(TPG):
                    sp.dma_start(types[t * NR:(t + 1) * NR, :].rearrange("p (g e) -> p g e", e=SUB),
                                 rows_t[:, t, :, :].to_broadcast([NR, U, SUB])).then_inc(types_loaded, 16)

            sp.wait_ge(types_stored, 32)
            load_types(0)
            sp.wait_ge(tiles_ready, 1)
            for k in range(2):
                sp.dma_start(tiles_dram[k, :].rearrange("(b t) -> b t", t=P), tiles_t[:, k, :]).then_inc(tiles_stored, 16)
            sp.wait_ge(tiles_stored, 32)
            sp.dma_start(tile_high, tiles_dram[1:2, :].to_broadcast([P, TALL])).then_inc(tile_high_back, 16)
            sp.wait_ge(keys_ready, 1)
            sp.dma_start(keys_dram.rearrange("(b p) f -> p b f", p=P),
                         keys_all.rearrange("p b e k -> p b (e k)")).then_inc(keys_stored, 16)
            sp.wait_ge(meta_ready, 1)
            for k in range(2):
                sp.dma_start(meta_dram[k, :].rearrange("(b g) -> b g", g=GB), meta_t[:, k, :]).then_inc(meta_stored, 16)
            sp.wait_ge(meta_stored, 32)
            sp.dma_start(meta[0:1, :, :], meta_dram.rearrange("(p k) g -> p k g", p=1)).then_inc(meta_back, 16)
            sp.dma_start(base_bc[:, :], meta_dram[0:1, :].to_broadcast([P, GALL])).then_inc(meta_back, 16)
            sp.wait_ge(table_rows_ready, 1)
            sp.dma_start(tile_rows, tiles_dram[:, 0:NT].rearrange("(p k) t -> p k t", p=1)).then_inc(tile_rows_back, 16)
            sp.wait_ge(starts_ready, 1)
            sp.dma_start(start_dram.rearrange("(p c) -> p c", c=WC), start_i[0:WP, :]).then_inc(starts_stored, 16)
            sp.wait_ge(starts_stored, 16)
            sp.dma_start(starts, start_dram.rearrange("(p w) -> p w", p=1)).then_inc(starts_back, 16)
            sp.wait_ge(types_hot_ready, 1)
            load_types(ST)
            for h in range(2):
                sp.dma_start(a_dram[HALVES + 1 + h, :, :],
                             a_half[:, h, :, :].rearrange("p b d -> p (b d)").bitcast(bf16)).then_inc(a_stored[h], 16)

            sp.wait_ge(starts_back, 16)

            keys_flat = keys_dram.rearrange("t f -> (t f)")
            regs = [sp.alloc_register(f"sp_start{n}") for n in range(WPS)]

            def load_keys(it, s):
                sp.wait_ge(hots_ready, it * WPS + (s + 1))
                first = sp.snap(regs[s], min_val=0, max_val=FULL_T * SUB + SUB)
                sp.dma_start(keys[:, s, :, :],
                             keys_flat[bass.ds(first * 2, P * WVIS * 2)].rearrange("(p v k) -> p v k", v=WVIS, k=2)
                             ).then_inc(keys_loaded[s], 16)

            def store_half(index, h):
                sp.dma_start(a_dram[bass.ds(index, 1), :, :].rearrange("a p n -> p (a n)"),
                             a_half[:, h, :, :].rearrange("p b d -> p (b d)").bitcast(bf16)).then_inc(a_stored[h], 16)

            with sp.Fori(0, STEPS) as it:
                sp.load(regs, starts[:, bass.ds(it * WPS, WPS)])
                for s in range(HW):
                    load_keys(it, s)
                sp.wait_ge(win_read, it * WPS + 2)
                store_half(it * 2, 1)
                for s in range(HW, WPS):
                    load_keys(it, s)
                sp.wait_ge(types_hot_ready, it + 2)
                load_types((it + 2) * ST)
                sp.wait_ge(win_read, it * WPS + (HW + 2))
                store_half(it * 2 + 1, 0)
            sp.wait_ge(win_read, STEPS * WPS + 2)
            store_half(HALVES, 1)

            sp.wait_ge(windows_over, 1)
            sp.dma_start(xb[:, 0:NBLK - 1, :], node_rows(x, 0, NBLK - 1)).then_inc(s_xb, 16)
            sp.dma_start(xb[0:NREST, NBLK - 1, :], x[(NBLK - 1) * P:N, :]).then_inc(s_xb, 16)

            def load_matrix(chunk, buf, halves=CH):
                sp.dma_start(a_buf[buf][:, 0:halves, :].bitcast(bf16),
                             a_dram[bass.ds(chunk * CH + 1, halves), :, :].rearrange("h p n -> p h n")
                             ).then_inc(a_loaded[buf], 16)

            for h in range(2):
                sp.wait_ge(a_stored[h], 16 * (STEPS + 1))
            sp.wait_ge(coef_done, STEPS + 1)
            sp.wait_ge(mm_done, GROUPS + U)
            load_matrix(0, 0)
            load_matrix(1, 1)
            sp.wait_ge(fault_known, 1)
            fault = sp.value_load(fault_i[0:1, 0:1], min_val=0, max_val=1)
            with sp.If(fault < 1):
                sp.wait_ge(idx_ready, GROUPS + U)
                load_matrix(2, 2)
                with sp.Fori(0, TRIPS - 1) as it:
                    for b in range(NBUF):
                        sp.wait_ge(conv_mm, it * NBUF + (b + 1))
                        load_matrix((it + 1) * NBUF + b, b)
                sp.wait_ge(conv_mm, (TRIPS - 1) * NBUF + 1)
                load_matrix(FULLC, 0, RESTH)
                with sp.Fori(0, TRIPS - 1) as it:
                    for n in range(NBUF):
                        b = (NBUF - n) % NBUF
                        sp.wait_ge(conv_mm, it * NBUF + (FULLC + 2 + n))
                        load_matrix(it * -NBUF + (FULLC - NBUF - n), b)
                sp.wait_ge(conv_mm, FULLC + 2 + NBUF * (TRIPS - 1))
                load_matrix(0, 0)
            with sp.Else():
                for b in range(2):
                    sp.wait_ge(a_loaded[b], 16)
            sp.nop()

        @block.gpsimd
        def _(pool):
            pool.memset(no_type[:, :], -1).then_inc(pool_consts, 1)
            pool.memset(neg_exact[:, :], -float(EXACT)).then_inc(pool_consts, 1)
            pool.memset(ones[:, :], 1.0).then_inc(pool_consts, 1)
            pool.iota(iota_i[:, :], [[1, WIN]], base=0, channel_multiplier=0).then_inc(pool_consts, 1)
            pool.iota(rel_i[:, :], [[0, 1]], base=0, channel_multiplier=1).then_inc(pool_consts, 1)
            pool.iota(shift_i[:, :], [[-WIN, XMAX]], base=-WIN, channel_multiplier=0).then_inc(pool_consts, 1)
            pool.iota(thr_i[:, :], [[WD, WC]], base=0, channel_multiplier=WD * WC).then_inc(pool_consts, 1)
            pool.iota(wbase_i[:, :], [[WCOL, NW]], base=0, channel_multiplier=0).then_inc(pool_consts, 1)
            pool.iota(iota_w_i[:, :], [[1, WCOL]], base=0, channel_multiplier=0).then_inc(pool_consts, 1)
            pool.memset(ident[:, :], 0.0).then_inc(pool_consts, 1)
            pool.memset(from_parts[:, :], 0.0).then_inc(pool_consts, 1)
            pool.wait_ge(pool_consts, 11)
            pool.affine_select(out=ident[:, :], in_=ident[:, :], compare_op=ALU.not_equal, fill=1.0, base=0,
                               pattern=[[-1, P]], channel_multiplier=1).then_inc(pool_consts, 1)
            for n, (base, wide) in enumerate(((0, HID + 1), (-(HID + 1), HID), (-(2 * HID + 1), HID))):
                if n:
                    pool.wait_ge(from_parts_step, n)
                ins = pool.affine_select(out=from_parts[:, 0:wide], in_=from_parts[:, 0:wide],
                                         compare_op=ALU.not_equal, fill=1.0, base=base,
                                         pattern=[[-1, wide]], channel_multiplier=1)
                ins.then_inc(from_parts_step if n < 2 else pool_consts, 1)
            pool.memset(faults[:, :], 0.0).then_inc(pool_consts, 1)
            pool.wait_ge(tile_cnt_ready, 1)
            pool.wait_ge(keys_stored, 16)
            for c in range(WC):
                pool.indirect_dma_start(
                    key_rows[:, c, :], None, keys_dram,
                    bass.IndirectOffsetOnAxis(ap=tile_cnt_i[0:WP, c:c + 1].bitcast(u32), axis=0),
                ).then_inc(key_rows_in, 16)
            pool.wait_ge(table_stored, 16)

            def gathers(k, ready):
                with pool.Fori(0, STEPS) as it:
                    for u in range(U):
                        pool.wait_ge(ready, it * U + (GROUPS * max(k - 1, 0) + u + 1))
                        pool.wait_ge(mm_done, it * U + (GROUPS * k + u + 1))
                        pool.sem_inc(gathers_begun, 1)
                        for t in range(TPG):
                            pool.indirect_dma_start(
                                rows[:, u, t, :], None, tables[k],
                                bass.IndirectOffsetOnAxis(ap=idx[:, u, t:t + 1].bitcast(u32), axis=0),
                            ).then_inc(gathered[u], 16)

            gathers(0, idx_ready)
            pool.wait_ge(fault_known, 1)
            fault = pool.value_load(fault_i[0:1, 0:1], min_val=0, max_val=1)
            with pool.If(fault > 0):
                for k in (1, 2):
                    pool.wait_ge(table_stored, 32 * k + 16)
                    gathers(k, idx_ready_sage)
            pool.nop()

        @block.scalar
        def _(act):
            act.dma_start(xa, x.rearrange("(p j) d -> p j d", p=XP)).then_inc(s_xa, 16)
            act.wait_ge(s_pad, 4)
            for t in range(TPG):
                act.dma_start(comp_f[t * NR:(t + 1) * NR, t * NB:(t + 1) * NB], w_comp).then_inc(s_comp, 16)
            for b in range(NB):
                act.dma_start(basis_sb[(b // 2) * D:(b // 2 + 1) * D, b % 2, :], w_basis[b, :, :]).then_inc(s_consts, 16)
            act.dma_start(w1_sb[:, 0:HID], w1_l).then_inc(s_consts, 16)
            act.dma_start(w1_sb[:, HID:2 * HID], w1_r).then_inc(s_consts, 16)
            for first in (0, HID + 1, 2 * HID + 1):
                act.dma_start(w2l_sb[first:first + HID, :], w2_l).then_inc(s_consts, 16)
            act.dma_start(w2r_sb[:, :], w2_r).then_inc(s_consts, 16)
            for vec, tile, n in ((bias, bias_bc, D), (b1, b1_bc, HID), (b2, b2_bc, D)):
                act.dma_start(tile[:, :], vec.rearrange("(a n) -> a n", a=1).to_broadcast([P, n])).then_inc(s_consts, 16)
            act.sem_inc(win_read, 2)
            act.sem_inc(conv_read, NBUF)
            for n in range(8):
                tile = src_cols if n < 4 else wgt_cols
                q, w = (n % 4) * 512, min(512, TALL - (n % 4) * 512)
                act.wait_ge(tr_done, n + 1)
                act.activation(tile[:, q:q + w], ps[:, n % 6, 0:w], ACT.Copy).then_inc(cols_copied, 1)
            act.wait_ge(cols_copied, 8)

            def copy_idx(tile0, u, ready):
                act.activation(idx[:, u, :], src_cols[:, bass.ds(tile0, TPG)], ACT.Copy).then_inc(ready, 1)

            for u in range(U):
                copy_idx(u * TPG, u, idx_ready)
            act.wait_ge(var_ready, 1)
            act.activation(stat[0:XP, 3, :], stat[0:XP, 2, :], ACT.Sqrt).then_inc(std_ready, 1)
            act.wait_ge(table_rows_ready, 1)
            act.dma_start(tables[0].rearrange("(p j) d -> p j d", p=XP), xc[0:XP, :, :]).then_inc(table_stored, 16)
            act.wait_ge(pool_consts, POOL_CONSTS)
            with act.Fori(0, STEPS) as it:
                for u in range(U):
                    for j in range(2):
                        s = 2 * u + j
                        act.wait_ge(win_mm, it * WPS + (s + 3))
                        if s % HW == 0:
                            act.wait_ge(a_stored[s // HW], it * 16 + 16)
                        act.sem_inc(copies_begun, 1)
                        win = ps[:, 3 + j, 0:WCOL]
                        act.activation(a_half[:, s // HW, :, (s % HW) * WD:(s % HW + 1) * WD].rearrange("p b d -> p d b"),
                                       win.rearrange("p (d b) -> p d b", b=NBLK), ACT.Copy, saturate=True)
                        act.wait_ge(win_read, it * WPS + (s + 2))
                        act.activation(above[:, :], win, ACT.Relu, bias=neg_exact[:, 0:1],
                                       accum_out=above_sum[:, bass.ds(it * WPS + s, 1)]).then_inc(win_read, 1)
                    act.wait_ge(mm_done, it * U + (U + u + 1))
                    copy_idx((it + 1) * ST + u * TPG, u, idx_ready)
            act.wait_ge(var_ready, 2)
            act.activation(stat[:, 3, 0:NBLK], stat[:, 2, 0:NBLK], ACT.Sqrt).then_inc(std_ready, 1)
            act.wait_ge(fault_known, 1)
            fault = act.value_load(fault_i[0:1, 0:1], min_val=0, max_val=1)

            def copy_sums(n, bank, col, wide):
                act.wait_ge(conv_mm, n)
                act.activation(acc[0:H3W, 0, bass.ds(col, wide)], ps[0:H3W, bank, 0:wide],
                               ACT.Copy).then_inc(conv_read, 1)

            with act.If(fault < 1):
                with act.Fori(0, TRIPS) as it:
                    for b in range(NBUF):
                        copy_sums(it * NBUF + (b + 1), b, (it * NBUF + b) * 512, 512)
                copy_sums(FULLC + 1, NBUF, FULLC * 512, RESTH * HDST)
                copy_sums(FULLC + 2, NBUF, FULLC * 512, RESTH * HDST)
                with act.Fori(0, TRIPS) as it:
                    for n in range(NBUF):
                        copy_sums(it * NBUF + (FULLC + 3 + n), NBUF - 1 - n,
                                  it * (-NBUF * 512) + (FULLC - 1 - n) * 512, 512)
            with act.Else():
                for k in (1, 2):
                    act.wait_ge(table_rows_ready, k + 1)
                    act.dma_start(node_rows(tables[k], 0, NBLK - 1), g_rows[:, 0:NBLK - 1, :]).then_inc(table_stored, 16)
                    act.dma_start(tables[k][(NBLK - 1) * P:N, :], g_rows[0:NREST, NBLK - 1, :]).then_inc(table_stored, 16)
                    with act.Fori(0, STEPS) as it:
                        for u in range(U):
                            act.wait_ge(mm_done, it * U + (GROUPS * k + u + 1))
                            copy_idx(it * ST + u * TPG, u, idx_ready_sage)
            act.wait_ge(table_rows_ready, 4)
            act.dma_start(node_rows(out, 0, NBLK - 1), g_rows[:, 0:NBLK - 1, :]).then_inc(s_out, 16)
            act.dma_start(out[(NBLK - 1) * P:N, :], g_rows[0:NREST, NBLK - 1, :]).then_inc(s_out, 16)
            act.wait_ge(s_out, 32)

        @block.vector
        def _(dve):
            steps = [0]

            def link(ins):
                steps[0] += 1
                ins.then_inc(dve_step, 1)
                dve.wait_ge(dve_step, steps[0])

            dve.memset(dst_rows[:, BLK - 1, :], PAD).then_inc(s_pad, 1)
            dve.memset(src_rows[:, BLK - 1, :], 0).then_inc(s_pad, 1)
            dve.memset(wgt_rows[:, BLK - 1, :], 0.0).then_inc(s_pad, 1)
            dve.memset(w2l_sb[:, :], 0.0)
            link(dve.memset(comp_f[:, :], 0.0))
            dve.nop().then_inc(s_pad, 1)
            dve.sem_inc(hots_ready, WPS)

            def norm(rows_in, mid, res, p, n, waits):
                st = stat[0:p, :, 0:n]
                link(dve.tensor_reduce(st[:, 0, :], rows_in, axis=AX, op=ALU.add))
                link(dve.tensor_scalar(st[:, 0, :], st[:, 0, :], 1.0 / D, None, ALU.mult))
                mean = st[:, 0, :].unsqueeze(2).to_broadcast([p, n, D])
                link(dve.tensor_tensor(mid, rows_in, mean, ALU.subtract))
                link(dve.tensor_tensor(res, mid, mid, ALU.mult))
                link(dve.tensor_reduce(st[:, 1, :], res, axis=AX, op=ALU.add))
                dve.tensor_scalar(st[:, 2, :], st[:, 1, :], 1.0 / D, EPS, ALU.mult, ALU.add).then_inc(var_ready, 1)
                dve.wait_ge(std_ready, waits)
                link(dve.reciprocal(st[:, 1, :], st[:, 3, :]))
                scale = st[:, 1, :].unsqueeze(2).to_broadcast([p, n, D])
                return dve.scalar_tensor_tensor(out=res, in0=mid, scalar=0.0, in1=scale, op0=ALU.max, op1=ALU.mult)

            dve.wait_ge(s_dst, 48)
            link(dve.tensor_copy(dst_rows_f, dst_rows))
            dve.tensor_reduce(low_high[:, 0, 0:BLK], dst_rows_f, axis=AX, op=ALU.min)
            dve.tensor_reduce(low_high[:, 1, 0:BLK], dst_rows_f, axis=AX, op=ALU.max)
            last = dst_rows_f[:, BLK - 1, :]
            fill_off = scratch[:, 0:SUB]
            link(dve.tensor_scalar(fill_off, last, float(PAD), -10.0 * PAD, ALU.is_ge, ALU.mult))
            link(dve.tensor_tensor(fill_off, fill_off, last, ALU.add))
            link(dve.tensor_copy(low_high[:, 2, 0:BLK], low_high[:, 1, 0:BLK]))
            link(dve.tensor_reduce(low_high[:, 2, BLK - 1:BLK], fill_off, axis=AX, op=ALU.max))
            dve.nop().then_inc(low_high_ready, 1)
            dve.wait_ge(s_src, 48)
            blk_of = scratch_i.rearrange("p (b e) -> p b e", e=SUB)
            dve.tensor_copy(src_rows_f, src_rows)
            link(dve.tensor_single_scalar(blk_of, src_rows, 7, ALU.logical_shift_right))
            dve.nop().then_inc(rows_cast, 1)
            dve.scalar_tensor_tensor(out=keys_all[:, :, :, 0], in0=dst_rows_f, scalar=float(NBLK), in1=blk_of,
                                     op0=ALU.mult, op1=ALU.add)
            link(dve.scalar_tensor_tensor(out=keys_all[:, :, :, 1], in0=blk_of, scalar=-float(P), in1=src_rows_f,
                                          op0=ALU.mult, op1=ALU.add))
            dve.nop().then_inc(keys_ready, 1)
            dve.wait_ge(low_high_tr, 1)
            tr = ps[0:BLK, 6, 0:3 * P].rearrange("b (k n) -> b k n", k=3)
            link(dve.tensor_copy(tiles_t[:, :, :], tr[:, 0:2, :]))
            dve.nop().then_inc(tiles_ready, 1)
            by_group = tr.rearrange("b k (g t) -> b k g t", t=TPG)
            dve.tensor_reduce(low_high_t[:, 0, :], by_group[:, 0, :, :], axis=AX, op=ALU.min)
            link(dve.tensor_reduce(low_high_t[:, 1, :], by_group[:, 2, :, :], axis=AX, op=ALU.max))
            link(dve.tensor_scalar(low_high_t[:, 0, :], low_high_t[:, 0, :], float(N - 1), None, ALU.min))
            link(dve.tensor_tensor(low_high_t[:, 1, :], low_high_t[:, 1, :], low_high_t[:, 0, :], ALU.subtract))
            link(dve.tensor_scalar(low_high_t[:, 1, :], low_high_t[:, 1, :], 0.0, -(WIN - 1) / 2, ALU.max, ALU.add))
            link(dve.tensor_scalar(low_high_t[:, 1, :], low_high_t[:, 1, :], 1.0 / WIN, None, ALU.mult))
            link(dve.tensor_copy(meta_t[:, :, :], low_high_t[:, :, :]))
            dve.nop().then_inc(meta_ready, 1)

            dve.wait_ge(s_xa, 16)
            mid = acc[0:XP, 0, 0:XN * D].rearrange("p (j d) -> p j d", d=D)
            link(norm(xa, mid, xc[0:XP, :, :], XP, XN, 1))
            dve.nop().then_inc(table_rows_ready, 1)

            dve.wait_ge(pool_consts, POOL_CONSTS)
            link(dve.tensor_copy(thr[:, 0, :], thr_i[:, :]))
            link(dve.tensor_scalar(thr[:, 1, :], thr[:, 0, :], float(NBLK), None, ALU.mult))
            dve.wait_ge(tile_high_back, 16)
            for c in range(WC):
                link(dve.tensor_scalar(scratch, tile_high, thr[:, 0, c:c + 1], None, ALU.is_lt, ALU.add,
                                       accum_out=tile_cnt[:, c:c + 1]))
            link(dve.tensor_copy(tile_cnt_i[:, :], tile_cnt[:, :]))
            dve.nop().then_inc(tile_cnt_ready, 1)
            dve.tensor_copy(iota[:, :], iota_i[:, :])
            dve.tensor_copy(shift[:, :], shift_i[:, :])
            dve.tensor_copy(wbase[:, :], wbase_i[:, :])
            dve.tensor_copy(iota_l[:, :], iota_w_i[:, 0:P])
            dve.tensor_copy(iota_q[:, :], iota_w_i[:, :])
            link(dve.tensor_single_scalar(rel_i[:, :], rel_i[:, :], NR - 1, ALU.bitwise_and))
            link(dve.tensor_copy(rel_of_p[:, :], rel_i[:, :]))
            for n in range(4):
                q, w = n * 512, min(512, TALL - n * 512)
                dve.wait_ge(tr_done, n + 9)
                dve.tensor_copy(dst_rel[:, q:q + w], ps[:, (n + 8) % 6, 0:w]).then_inc(dst_copied, 1)
            dve.wait_ge(dst_copied, 4)
            dve.wait_ge(key_rows_in, 16 * WC)
            for c in range(WC):
                link(dve.tensor_scalar(scratch[0:WP, 0:SUB], key_rows[:, c, 0:2 * SUB:2], thr[0:WP, 1, c:c + 1], None,
                                       ALU.is_lt, ALU.add, accum_out=edge_cnt[0:WP, c:c + 1]))
            link(dve.scalar_tensor_tensor(out=edge_cnt[0:WP, :], in0=tile_cnt[0:WP, :], scalar=float(SUB),
                                          in1=edge_cnt[0:WP, :], op0=ALU.mult, op1=ALU.add))
            link(dve.tensor_copy(start_i[0:WP, :], edge_cnt[0:WP, :]))
            dve.nop().then_inc(starts_ready, 1)

            def count_below(into, a, b, bound, tmp):
                link(dve.tensor_tensor(tmp, a, b, ALU.subtract))
                link(dve.tensor_scalar(tmp, tmp, bound, None, ALU.is_lt, ALU.add, accum_out=into))

            tmp = scratch[:, 0:BLK * (SUB - 1)].rearrange("p (b e) -> p b e", b=BLK)
            count_below(faults[:, 0:1], dst_rows_f[:, :, 1:SUB], dst_rows_f[:, :, 0:SUB - 1], 0.0, tmp)
            dve.wait_ge(tile_rows_back, 16)
            count_below(faults[0:1, 2:3], tile_rows[:, 0, 1:NT], tile_rows[:, 1, 0:NT - 1], 0.0, scratch[0:1, 0:NT - 1])
            dve.wait_ge(meta_back, 32)
            groups_of = dst_rel.rearrange("p (g t) -> p g t", t=TPG)
            link(dve.tensor_tensor(groups_of, groups_of,
                                   base_bc[:, :].unsqueeze(2).to_broadcast([P, GALL, TPG]), ALU.subtract))
            dve.wait_ge(s_comp, 16 * TPG)
            link(dve.tensor_copy(comp_parts[:, 0, :], comp_f[:, :]))
            link(dve.tensor_tensor(comp_r[:, :], comp_f[:, :], comp_parts[:, 0, :], ALU.subtract))
            link(dve.tensor_copy(comp_parts[:, 1, :], comp_r[:, :]))
            link(dve.tensor_tensor(comp_r[:, :], comp_r[:, :], comp_parts[:, 1, :], ALU.subtract))
            link(dve.tensor_copy(comp_parts[:, 2, :], comp_r[:, :]))
            dve.nop().then_inc(comp_ready, 1)
            dve.wait_ge(starts_back, 16)
            lens = scratch[32:33, 0:NW - 1]
            link(dve.tensor_tensor(lens, starts[:, 1:NW], starts[:, 0:NW - 1], ALU.subtract))
            link(dve.tensor_scalar(lens, lens, float(P * WVIS), None, ALU.is_gt, ALU.add, accum_out=faults[32:33, 3:4]))
            link(dve.tensor_scalar(faults[32:33, 4:5], starts[:, NW - 1:NW], float(E - P * WVIS), None, ALU.is_lt))
            dve.wait_ge(keys_stored, 16)
            dve.memset(acc[:, :, :], 0.0)

            def types_to_hot(n_expr):
                dve.wait_ge(types_loaded, n_expr * (16 * TPG))
                dve.tensor_scalar(types_hot[:, :], types[:, :], rel_of_p[:, 0:1], None,
                                  ALU.is_equal).then_inc(types_hot_ready, 1)

            def coefficients(n_expr, tile0):
                dve.wait_ge(coef_mm, n_expr)
                dve.tensor_tensor(coef[:, bass.ds(tile0, ST), :],
                                  ps[:, 5, 0:ST * NB].rearrange("p (t b) -> p t b", b=NB),
                                  wgt_cols[:, bass.ds(tile0, ST)].unsqueeze(2).to_broadcast([P, ST, NB]),
                                  ALU.mult).then_inc(coef_done, 1)

            dve.wait_ge(cols_copied, 8)
            types_to_hot(1)
            coefficients(1, 0)

            iota_w = iota[:, :].unsqueeze(1).to_broadcast([P, TPG, WIN])

            def weigh(into, hots, cf):
                return dve.tensor_tensor(into, hots.unsqueeze(2).to_broadcast([P, TPG, NB, WIN]),
                                         cf.unsqueeze(3).to_broadcast([P, TPG, NB, WIN]), ALU.mult)

            x_done = dve.alloc_register("dve_x_done")
            x_steps = dve.alloc_register("dve_x_steps")
            x_base = dve.alloc_register("dve_x_base")
            prev = dve.alloc_register("dve_prev_base")
            dve.reg_mov(x_done, 0)
            dve.reg_mov(x_steps, 0)
            regs = [dve.alloc_register(f"dve_meta{n}") for n in range(2 * U)]

            def window_keys(it, u):
                for j in range(2):
                    dve.wait_ge(keys_loaded[2 * u + j], it * 16 + 16)
                dve.tensor_tensor(key_rel[:, u % 2, :, :], keys[:, 2 * u:2 * u + 2, :, 0],
                                  wbase[:, bass.ds(it * WPS + 2 * u, 2)].unsqueeze(2).to_broadcast([P, 2, WVIS]),
                                  ALU.subtract).then_inc(key_rel_ready, 1)

            def window_hots(it, u, j):
                dve.wait_ge(win_mm, it * WPS + (2 * u + j + 1))
                if j == 0:
                    dve.wait_ge(key_rel_ready, it * U + (u + 1))
                for v in range(WVIS):
                    dve.tensor_scalar(row_hot[:, j, v, :], iota_l[:, :], keys[:, 2 * u + j, v, 1:2], None,
                                      ALU.is_equal)
                    ins = dve.tensor_scalar(col_hot[:, j, v, :], iota_q[:, :], key_rel[:, u % 2, j, v:v + 1], None,
                                            ALU.is_equal)
                ins.then_inc(hots_ready, 1)

            def aggregate(k):
                parts, nb = (P, 2) if k == 0 else (D, 1)
                dve.reg_mov(prev, 0)
                dve.memset(ps[:, 1, 0:2 * WIN], 0.0).then_inc(stand_in, 1)
                dve.wait_ge(stand_in, k + 1)
                if k == 0:
                    dve.sem_inc(psum_free, 1)

                def add_sums(slot, base, i_expr):
                    into = acc[0:parts, 0:nb, bass.ds(base, WIN)]
                    dve.wait_ge(mm_done, i_expr + (GROUPS * k + U))
                    dve.wait_ge(psum_free, i_expr + (GROUPS + 1) * k + 1)
                    dve.tensor_tensor(into, into, ps[0:parts, slot, 0:nb * WIN].rearrange("p (b w) -> p b w", w=WIN),
                                      ALU.add).then_inc(psum_free, 1)

                with dve.Fori(0, STEPS) as it:
                    dve.load(regs[0:U], meta[0:1, 0, bass.ds(it * U, U)])
                    dve.load(regs[U:2 * U], meta[0:1, 1, bass.ds(it * U, U)])
                    for u in range(U):
                        i = it * U + u
                        tile0 = it * (U * TPG) + u * TPG
                        extra = dve.snap(regs[U + u], min_val=0, max_val=XMAX - 1)
                        if k == 0 and u == 0:
                            types_to_hot(it + 2)
                        if k == 0:
                            window_keys(it, u)
                        rel = dst_rel[:, bass.ds(tile0, TPG)]
                        cf = coef[:, bass.ds(tile0, TPG), :]
                        dve.tensor_tensor(hot[:, u % 2, :, :], iota_w, rel.unsqueeze(2).to_broadcast([P, TPG, WIN]),
                                          ALU.is_equal).then_inc(onehot_ready if k == 0 else wts_ready, 1)
                        with dve.If(extra > 0):
                            dve.reg_mov(x_base, regs[u])
                            with dve.Fori(0, extra) as j:
                                dve.tensor_scalar(x_rel[:, :], rel, shift[:, bass.ds(j, 1)], None,
                                                  ALU.add).then_inc(x_step, 1)
                                dve.wait_ge(x_step, dve.snap(x_steps) + 1)
                                ins = dve.tensor_tensor(x_hot[:, :, :], iota_w,
                                                        x_rel[:, :].unsqueeze(2).to_broadcast([P, TPG, WIN]),
                                                        ALU.is_equal)
                                if k == 0:
                                    ins.then_inc(x_step, 1)
                                    dve.wait_ge(x_step, dve.snap(x_steps) + 2)
                                    weigh(x_wts[:, :, :, :], x_hot[:, :, :], cf).then_inc(x_wts_ready, 1)
                                else:
                                    ins.then_inc(x_wts_ready, 1)
                                dve.reg_add(x_base, x_base, WIN)
                                into = acc[0:parts, 0:nb,
                                           bass.ds(dve.snap(x_base, min_val=0, max_val=ACCW - WIN), WIN)]
                                dve.wait_ge(x_mm_done, dve.snap(x_done) + 1)
                                dve.wait_ge(psum_free, i + (GROUPS + 1) * k + 1)
                                dve.tensor_tensor(into, into,
                                                  ps[0:parts, 2, 0:nb * WIN].rearrange("p (b w) -> p b w", w=WIN),
                                                  ALU.add).then_inc(x_step, 1)
                                dve.reg_add(x_done, x_done, 1)
                                dve.reg_add(x_steps, x_steps, 3 if k == 0 else 2)
                                dve.wait_ge(x_step, dve.snap(x_steps))
                        if k == 0:
                            window_hots(it, u, 0)
                            dve.wait_ge(onehot_ready, i + 1)
                            weigh(wts[:, u % 2, :, :, :], hot[:, u % 2, :, :], cf).then_inc(wts_ready, 1)
                            window_hots(it, u, 1)
                        if k == 0 and u == 2:
                            coefficients(it + 2, (it + 1) * ST)
                        add_sums((u + 1) % 2, dve.snap(prev, min_val=0, max_val=N - 1), i)
                        dve.reg_mov(prev, regs[u])
                add_sums(1, dve.snap(prev, min_val=0, max_val=N - 1), GROUPS)
                dve.wait_ge(psum_free, (GROUPS + 1) * (k + 1) + 1)
                dve.nop().then_inc(sums_ready, 1)

            def banks(width, p=P):
                return ps[0:p, 0:-(-NBLK // 8), :].rearrange("p k (b d) -> p (k b) d", d=D)[:, 0:NBLK, 0:width]

            def per_node(v, w):
                return v.unsqueeze(2).to_broadcast([P, NBLK, w])

            def per_feature(v, w):
                return v.unsqueeze(1).to_broadcast([P, NBLK, w])

            def transposed(n, p, into):
                for q in range(-(-NBLK // 4)):
                    w = min(4, NBLK - 4 * q) * P
                    dve.wait_ge(node_mm, n + q + 1)
                    dve.tensor_copy(into[:, q * 512:q * 512 + w], ps[0:p, q % 8, 0:w]).then_inc(ps_read, 1)

            NQ = -(-NBLK // 4)
            xb_v, g_v, xc_v = xb[:, :, :], g_rows, xc[:, 0:NBLK, :]

            def split(k):
                v, rest = g_v[:, :, 0:HID], centred[:, :, 0:HID]
                hi, mid_, lo = (parts3[:, :, a:a + HID] for a in (0, HID + 1, 2 * HID + 1))
                link(dve.tensor_copy(hi, v))
                link(dve.tensor_tensor(rest, v, hi, ALU.subtract))
                link(dve.tensor_copy(mid_, rest))
                link(dve.tensor_tensor(rest, rest, mid_, ALU.subtract))
                link(dve.tensor_copy(lo, rest))
                link(dve.memset(parts3[:, :, HID:HID + 1], 1.0))
                dve.nop().then_inc(parts_ready, 1)

            def sage_sums(k, fault):
                with dve.If(fault > 0):
                    aggregate(k)
                with dve.Else():
                    dve.wait_ge(conv_read, NBUF + (FULLC + 1) * k)
                    dve.nop().then_inc(sums_ready, 1)
                dve.nop()

            aggregate(0)
            dve.wait_ge(win_read, NW + 2)
            dve.memset(xb[:, NBLK - 1, :], 0.0).then_inc(windows_over, 1)
            link(dve.tensor_reduce(faults[:, 1:2], above_sum[:, :], axis=AX, op=ALU.add))
            link(dve.tensor_reduce(faults[:, 7:8], faults[:, 0:5], axis=AX, op=ALU.add))
            dve.nop().then_inc(faults_in, 1)
            dve.wait_ge(faults_mm, 1)
            link(dve.tensor_scalar(faults[0:1, 6:7], ps[0:1, 7, 0:1], 1.0, None, ALU.min))
            link(dve.tensor_copy(fault_i[:, :], faults[0:1, 6:7]))
            dve.nop().then_inc(fault_known, 1)
            fault = dve.value_load(fault_i[0:1, 0:1], min_val=0, max_val=1)
            dve.wait_ge(s_consts, CONST_DMAS)
            dve.wait_ge(s_xb, 32)
            dve.wait_ge(node_mm, 1)
            link(dve.tensor_tensor(xc_v, banks(D), per_feature(bias_bc[:, :], D), ALU.add))
            link(dve.scalar_tensor_tensor(out=xb_v, in0=xc_v, scalar=0.0, in1=xb_v, op0=ALU.max, op1=ALU.add))
            link(norm(xb_v, centred, xc_v, P, NBLK, 2))
            dve.nop().then_inc(node_in, 1)
            transposed(1, D, acc[0:D, 1, 0:NBLK * P])
            dve.wait_ge(ps_read, NQ)
            dve.memset(acc[:, 0, :], 0.0)
            dve.nop().then_inc(node_in, 1)
            link(dve.memset(g_v[:, :, HID:D], 0.0))
            link(dve.memset(g_v[:, :, HID:HID + 1], 1.0))
            dve.wait_ge(node_mm, 2 + NQ)
            link(dve.tensor_copy(g_v[:, :, 0:HID], banks(HID)))
            dve.nop().then_inc(table_rows_ready, 1)
            right1 = xc_v[:, :, 0:HID]
            link(dve.tensor_tensor(right1, banks(2 * HID)[:, :, HID:2 * HID], per_feature(b1_bc[:, :], HID), ALU.add))
            split(1)
            sage_sums(1, fault)
            dve.wait_ge(node_mm, 3 + NQ)
            link(dve.tensor_scalar(recip_cnt[:, :].unsqueeze(2), banks(HID + 1)[:, :, HID:HID + 1], 1.0, None, ALU.max))
            link(dve.reciprocal(recip_cnt[:, :], recip_cnt[:, :]))
            hid = g_v[:, :, 0:HID]
            link(dve.tensor_tensor(hid, banks(HID), per_node(recip_cnt[:, :], HID), ALU.mult))
            link(dve.tensor_tensor(hid, hid, right1, ALU.add))
            link(dve.tensor_scalar(hid, hid, 0.0, None, ALU.max))
            dve.nop().then_inc(table_rows_ready, 1)
            dve.nop().then_inc(node_in, 1)
            transposed(3 + NQ, HID, acc[0:HID, 1, 0:NBLK * P])
            dve.wait_ge(ps_read, 2 * NQ)
            link(dve.memset(acc[:, 0, :], 0.0))
            dve.nop().then_inc(node_in, 1)
            dve.wait_ge(node_mm, 4 + 2 * NQ)
            link(dve.tensor_tensor(xb_v, xb_v, banks(D), ALU.add))
            link(dve.tensor_tensor(xb_v, xb_v, per_feature(b2_bc[:, :], D), ALU.add))
            split(2)
            sage_sums(2, fault)
            dve.wait_ge(node_mm, 5 + 2 * NQ)
            link(dve.tensor_tensor(g_v, banks(D), per_node(recip_cnt[:, :], D), ALU.mult))
            link(dve.tensor_tensor(g_v, g_v, xb_v, ALU.add))
            dve.nop().then_inc(table_rows_ready, 1)

        @block.tensor
        def _(pe):
            pe.wait_ge(pool_consts, POOL_CONSTS)
            pe.wait_ge(low_high_ready, 1)
            for k in range(3):
                ins = pe.transpose(ps[0:BLK, 6, k * P:(k + 1) * P], low_high[:, k, 0:BLK], ident[:, :])
            ins.then_inc(low_high_tr, 1)
            pe.wait_ge(rows_cast, 1)
            for n in range(12):
                tile = (src_rows_f, wgt_rows, dst_rows_f)[n // 4]
                if n == 4:
                    pe.wait_ge(s_wgt, 48)
                if n >= 6:
                    pe.wait_ge(cols_copied, n - 5)
                for b in range(4 * (n % 4), min(4 * (n % 4) + 4, BLK)):
                    ins = pe.transpose(ps[:, n % 6, (b % 4) * P:(b % 4 + 1) * P], tile[:, b, :], ident[:, :])
                ins.then_inc(tr_done, 1)
            pe.wait_ge(dst_copied, 4)
            pe.wait_ge(cols_copied, 8)
            pe.sem_inc(mm_done, U)
            pe.sem_inc(win_mm, 2)

            def type_rows(n_expr, done_before):
                pe.wait_ge(types_hot_ready, n_expr)
                if done_before is not None:
                    pe.wait_ge(coef_done, done_before)
                for g in range(U):
                    for part in range(3):
                        ins = pe.matmul(ps[:, 5, g * TPG * NB:(g + 1) * TPG * NB],
                                        types_hot[:, g * SUB:(g + 1) * SUB], comp_parts[:, part, :],
                                        start=part == 0, stop=part == 2)
                ins.then_inc(coef_mm, 1)

            def window(it, u, j):
                pe.wait_ge(hots_ready, it * WPS + (WPS + 2 * u + j + 1))
                pe.wait_ge(win_read, it * WPS + (2 * u + j + 1))
                for v in range(WVIS):
                    ins = pe.matmul(ps[:, 3 + j, 0:WCOL], row_hot[:, j, v, :], col_hot[:, j, v, :],
                                    start=v == 0, stop=v == WVIS - 1)
                ins.then_inc(win_mm, 1)

            pe.wait_ge(comp_ready, 1)
            type_rows(1, None)
            x_seen = pe.alloc_register("pe_x_seen")
            pe.reg_mov(x_seen, 0)
            regs = [pe.alloc_register(f"pe_extra{n}") for n in range(U)]

            def products(slot, hots, weights, k, u):
                for t in range(TPG):
                    if k:
                        ins = pe.matmul(ps[0:D, slot, 0:WIN], rows[:, u, t, :], hots[:, t, :],
                                        start=t == 0, stop=t == TPG - 1)
                        continue
                    for half in range(2):
                        ins = pe.matmul(ps[half * D:(half + 1) * D, slot, 0:2 * WIN], rows[:, u, t, :],
                                        weights[:, t, 2 * half:2 * half + 2, :].rearrange("p b w -> p (b w)"),
                                        start=t == 0, stop=t == TPG - 1)
                return ins

            def aggregate(k):
                with pe.Fori(0, STEPS) as it:
                    pe.load(regs, meta[0:1, 1, bass.ds(it * U, U)])
                    for u in range(U):
                        i = it * U + u
                        if k == 0 and u == 0:
                            type_rows(it + 2, it + 1)
                        extra = pe.snap(regs[u], min_val=0, max_val=XMAX - 1)
                        with pe.If(extra > 0):
                            pe.wait_ge(gathered[u], it * (16 * TPG) + 16 * TPG * (STEPS * k + 1))
                            pe.sem_inc(extras_begun, 1)
                            with pe.Fori(0, extra):
                                pe.wait_ge(x_wts_ready, pe.snap(x_seen) + 1)
                                products(2, x_hot[:, :, :], x_wts[:, :, :, :], k, u).then_inc(x_mm_done, 1)
                                pe.reg_add(x_seen, x_seen, 1)
                        if k == 0:
                            window(it, u, 0)
                        pe.wait_ge(gathered[u], it * (16 * TPG) + 16 * TPG * (STEPS * k + 1))
                        pe.wait_ge(wts_ready, i + (GROUPS * k + 1))
                        pe.wait_ge(psum_free, i + ((GROUPS + 1) * k + 1))
                        products(u % 2, hot[:, u % 2, :, :], wts[:, u % 2, :, :, :], k, u).then_inc(mm_done, 1)
                        if k == 0:
                            window(it, u, 1)

            def from_sums(wide, rhs):
                for b in range(NBLK):
                    for h in range(len(rhs)):
                        k_rows = rhs[h].shape[0]
                        ins = pe.matmul(ps[:, b // 8, (b % 8) * D:(b % 8) * D + wide],
                                        acc[0:k_rows, h, b * P:(b + 1) * P], rhs[h],
                                        start=h == 0, stop=h == len(rhs) - 1)
                ins.then_inc(node_mm, 1)

            def transposes(tile, wide, read_before):
                for b in range(NBLK):
                    if b % 4 == 0 and b // 4 >= 8:
                        pe.wait_ge(ps_read, read_before + b // 4 - 7)
                    ins = pe.transpose(ps[0:wide, b // 4 % 8, (b % 4) * P:(b % 4 + 1) * P], tile[:, b, 0:wide],
                                       ident[:, :])
                    if b % 4 == 3 or b == NBLK - 1:
                        ins.then_inc(node_mm, 1)

            def from_transposed(p, rhs):
                for b in range(NBLK):
                    ins = pe.matmul(ps[:, b // 8, (b % 8) * D:(b % 8 + 1) * D], acc[0:p, 1, b * P:(b + 1) * P], rhs,
                                    start=True, stop=True)
                ins.then_inc(node_mm, 1)

            def dense(n, buf, bank, halves):
                pe.wait_ge(conv_read, n)
                pe.sem_inc(dense_begun, 1)
                for b in range(NBLK):
                    ins = pe.matmul(ps[0:H3W, bank, 0:halves * HDST], parts3[:, b, :],
                                    a_buf[buf][:, 0:halves, b * HDST:(b + 1) * HDST],
                                    start=b == 0, stop=b == NBLK - 1)
                ins.then_inc(conv_mm, 1)

            def sage_sums(k, fault):
                with pe.If(fault > 0):
                    aggregate(k)
                with pe.Else():
                    pe.wait_ge(parts_ready, k)
                    if k == 2:
                        dense(NBUF + FULLC + 1, 0, NBUF, RESTH)
                    with pe.Fori(0, TRIPS) as it:
                        for n in range(NBUF):
                            b = n if k == 1 else NBUF - 1 - n
                            loads = 1 if k == 1 else (TRIPS + 1 if b else TRIPS + 2) - (b > 0)
                            pe.wait_ge(a_loaded[b], it * 16 + 16 * loads)
                            dense(it * NBUF + (n + 1 if k == 1 else FULLC + 3 + n), b, b, CH)
                    if k == 1:
                        pe.wait_ge(a_loaded[0], 16 * (TRIPS + 1))
                        dense(FULLC + 1, 0, NBUF, RESTH)
                pe.nop()

            NQ = -(-NBLK // 4)
            pe.wait_ge(meta_back, 32)
            pe.wait_ge(s_consts, CONST_DMAS)
            aggregate(0)
            pe.wait_ge(faults_in, 1)
            pe.matmul(ps[0:1, 7, 0:1], faults[:, 7:8], ones[:, :], start=True, stop=True).then_inc(faults_mm, 1)
            pe.wait_ge(sums_ready, 1)
            from_sums(D, [basis_sb[:, 0, :], basis_sb[:, 1, :]])
            pe.wait_ge(fault_known, 1)
            fault = pe.value_load(fault_i[0:1, 0:1], min_val=0, max_val=1)
            pe.wait_ge(node_in, 1)
            transposes(xc, D, 0)
            pe.wait_ge(node_in, 2)
            from_transposed(D, w1_sb[:, :])
            sage_sums(1, fault)
            pe.wait_ge(sums_ready, 2)
            from_sums(HID + 1, [from_parts[:, :]])
            pe.wait_ge(node_in, 3)
            transposes(g_rows, HID, NQ)
            pe.wait_ge(node_in, 4)
            from_transposed(HID, w2r_sb[:, :])
            sage_sums(2, fault)
            pe.wait_ge(sums_ready, 3)
            from_sums(D, [w2l_sb[:, :]])


_INS = ['x', 'src', 'dst', 'edge_type_32', 'edge_weight', 'L0_gnn_weight', 'L0_gnn_w_comp', 'L0_gnn_bias',
        'L1_gnn_W1_l', 'L1_gnn_b1', 'L1_gnn_W1_r', 'L1_gnn_W2_l', 'L1_gnn_b2', 'L1_gnn_W2_r']


def kernel(**inputs):
    import numpy as _np
    import concourse.bacc as _bacc
    from concourse import mybir as _mybir
    from concourse.bass_utils import run_bass_kernel_spmd as _run

    nc = _bacc.Bacc("TRN2", target_bir_lowering=False, num_devices=1)
    arrays, args = {}, []
    for name in _INS:
        a = _np.ascontiguousarray(inputs[name])
        arrays[f"in_{name}"] = a
        args.append(nc.dram_tensor(f"in_{name}", a.shape, _mybir.dt.from_np(a.dtype), kind="ExternalInput").ap())
    args.append(nc.dram_tensor("out_0", tuple(inputs['x'].shape), _mybir.dt.float32, kind="ExternalOutput").ap())
    gnn_kernel(nc, *args)
    r = _run(nc, [arrays], core_ids=[0])
    return r.results[0]["out_0"]
```

```python
from contextlib import ExitStack

import concourse.bass as bass
from concourse import mybir


def gnn_kernel(nc, x, src, dst, etype, weight_e, w_basis, w_comp, bias,
               w1_l, b1, w1_r, w2_l, b2, w2_r, out):
    f32, bf16, i32, u32 = mybir.dt.float32, mybir.dt.bfloat16, mybir.dt.int32, mybir.dt.uint32
    f16, f8 = mybir.dt.float16, mybir.dt.float8e4
    ALU, ACT, AX = mybir.AluOpType, mybir.ActivationFunctionType, mybir.AxisListType.X

    P = 128
    N, D = x.shape
    E = src.shape[0]
    NB, NR = w_basis.shape[0], w_comp.shape[0]
    HID = w1_l.shape[1]
    EPS = 1e-5
    TPG = 4
    WIN = 24
    U = 8
    SUB = 128
    BLK = -(-E // (P * SUB))
    FULL_T = E // SUB
    REST = E - FULL_T * SUB
    GROUPS = -(-(-(-E // SUB)) // (TPG * U)) * U
    STEPS = GROUPS // U
    GB = P // TPG
    GALL = BLK * GB
    TALL = BLK * P
    NBLK = -(-N // P)
    NREST = N - (NBLK - 1) * P
    ACCW = NBLK * P + WIN
    XMAX = -(-N // WIN)
    XP = 125
    XN = N // XP
    ST = U * TPG
    PAD = 1_000_000
    WD = 8
    WCOL = WD * NBLK
    WVIS = 3
    WPS = 2 * U
    NW = WPS * STEPS
    WP, WC = 112, NW // 112
    HW = WPS // 2
    HDST = HW * WD
    HALVES = 2 * STEPS
    EXACT = 16
    CH = 8
    FULLC = HALVES // CH
    RESTH = HALVES - FULLC * CH
    NBUF = 3
    TRIPS = FULLC // NBUF
    H3W = 3 * HID + 1
    assert XP * XN == N and NR * TPG == P and D == 64 and WP * WC == NW and NW * WD == NBLK * P
    assert CH * HDST == 512 and TRIPS * NBUF == FULLC and RESTH > 0

    tables = [nc.dram_tensor(f"table{k}", (N, D), f32).ap() for k in range(3)]
    meta_dram = nc.dram_tensor("meta_dram", (2, GALL), i32).ap()
    tiles_dram = nc.dram_tensor("tiles_dram", (2, TALL), f32).ap()
    keys_dram = nc.dram_tensor("keys_dram", (TALL, SUB * 2), f32).ap()
    start_dram = nc.dram_tensor("start_dram", (NW,), i32).ap()
    types_dram = nc.dram_tensor("types_dram", ((STEPS + 2) * ST * SUB,), i32).ap()
    early_dram = nc.dram_tensor("early_dram", (HALVES + 4, H3W, HDST), f32).ap()
    a_dram = nc.dram_tensor("a_dram", (HALVES + 3, P, NBLK * HDST // 2), bf16).ap()

    with ExitStack() as ctx:
        def sb(name, shape, dt):
            return ctx.enter_context(nc.sbuf_tensor(name, shape, dt))

        def sem(name):
            return ctx.enter_context(nc.semaphore(name))

        a_words = CH * NBLK * HDST // 4
        arena_rows = sb("arena_rows", [P, a_words], f32)

        def in_arena(arena, n, dt):
            return arena[:, n * TALL:(n + 1) * TALL].bitcast(dt)

        dst_rows, src_rows, wgt_rows = (in_arena(arena_rows, n, dt).rearrange("p (b e) -> p b e", e=SUB)
                                        for n, dt in enumerate((i32, i32, f32)))
        edge_rows_f = sb("edge_rows_f", [P, 2, BLK, SUB], f32)
        dst_rows_f, src_rows_f = edge_rows_f[:, 0, :, :], edge_rows_f[:, 1, :, :]
        arena_cols = sb("arena_cols", [P, a_words], f32)
        dst_rel, src_cols, wgt_cols = (in_arena(arena_cols, n, f32) for n in range(3))
        arena_coef = sb("arena_coef", [P, (STEPS + 1) * ST * NB], f32)
        coef = arena_coef[:, :].rearrange("p (t b) -> p t b", b=NB)
        low_high = sb("low_high", [P, 3, 16], f32)
        low_high_t = sb("low_high_t", [BLK, 2, GB], f32)
        meta_t = sb("meta_t", [BLK, 2, GB], i32)
        tables_i = sb("tables_i", [33, 2 * GALL], i32)
        meta = tables_i[0:1, :].rearrange("p (k g) -> p k g", k=2)
        starts = tables_i[32:33, 0:NW]
        shift = sb("shift", [P, XMAX], f32)
        types = sb("types", [P, U * SUB], i32)
        types_hot = sb("types_hot", [P, U * SUB], bf16)
        no_type = sb("no_type", [64, ((STEPS + 2) * ST * SUB - E) // 64], i32)
        thr_i = sb("thr_i", [P, WC], i32)
        thr = sb("thr", [P, 3, WC], f32)
        tile_cnt = sb("tile_cnt", [P, WC], f32)
        tile_cnt_i = sb("tile_cnt_i", [P, WC], i32)
        edge_cnt = sb("edge_cnt", [P, WC], f32)
        start_i = sb("start_i", [P, WC], i32)
        arena_win = sb("arena_win", [P, NW + WVIS * (P + WCOL) + WCOL // 2], f32)
        win_used = [0]

        def in_arena_win(n, dt):
            win_used[0] += n
            return arena_win[:, win_used[0] - n:win_used[0]].bitcast(dt)

        wbase = in_arena_win(NW, f32)
        iota_l = sb("iota_l", [P, P], f16)
        iota_q = sb("iota_q", [P, WCOL], f16)
        keys = sb("keys", [P, WPS, WVIS, 2], f32)
        key_rel = sb("key_rel", [P, 2, 2, WVIS], f32)
        row_hot = in_arena_win(WVIS * P, bf16).rearrange("p (j v c) -> p j v c", j=2, v=WVIS)
        col_hot = in_arena_win(WVIS * WCOL, bf16).rearrange("p (j v c) -> p j v c", j=2, v=WVIS)
        above = in_arena_win(WCOL // 2, bf16)
        a_half = edge_rows_f[:, :, :, :].rearrange("p a b e -> p (a b e)")[:, 0:NBLK * HDST // 2].bitcast(f8).rearrange(
            "p (h b d) -> p h b d", h=2, b=NBLK)
        above_sum = sb("above_sum", [P, NW], f32)
        base_bc = above_sum[:, 0:GALL].bitcast(i32)
        neg_exact = sb("neg_exact", [P, 1], f32)
        faults = sb("faults", [P, 8], f32)
        fault_i = sb("fault_i", [1, 1], i32)
        ones = sb("ones", [P, 1], f32)
        from_parts = sb("from_parts", [H3W, HID + 1], f32)
        rel_i = sb("rel_i", [P, 1], i32)
        rel_of_p = sb("rel_of_p", [P, 1], f32)
        comp_f = sb("comp_f", [P, TPG * NB], f32)
        comp_r = sb("comp_r", [P, TPG * NB], f32)
        comp_parts = sb("comp_parts", [P, 3, TPG * NB], bf16)
        ident = sb("ident", [P, P], f32)
        iota_i = sb("iota_i", [P, WIN], i32)
        iota = sb("iota", [P, WIN], f32)
        idx = sb("idx", [P, U, TPG], i32)
        rows = sb("rows", [P, U, TPG, D], f32)
        hot = sb("hot", [P, 2, TPG, WIN], f32)
        wts = sb("wts", [P, 2, TPG, NB, WIN], f32)
        x_rel = sb("x_rel", [P, TPG], f32)
        x_hot = sb("x_hot", [P, TPG, WIN], f32)
        x_wts = sb("x_wts", [P, TPG, NB, WIN], f32)
        acc = sb("acc", [P, 2, ACCW], f32)
        keys_all = arena_coef[:, 0:2 * TALL].rearrange("p (b e k) -> p b e k", e=SUB, k=2)
        scratch = arena_coef[:, 2 * TALL:3 * TALL]
        wbase_i = arena_coef[:, 3 * TALL:3 * TALL + NW].bitcast(i32)
        iota_w_i = arena_coef[:, 3 * TALL + NW:3 * TALL + NW + WCOL].bitcast(i32)
        tile_high = arena_win[:, NW:NW + TALL]
        shift_i = arena_rows[:, a_words - XMAX:a_words].bitcast(i32)
        rows_flat = rows[:, :, :, :].rearrange("p u t d -> p (u t d)")
        blk_of_i = rows_flat[:, 2 * P:2 * P + TALL].bitcast(i32)
        tiles_t = rows_flat[0:BLK, 0:2 * P].rearrange("p (k t) -> p k t", k=2)
        key_rows = arena_rows[0:WP, 0:WC * SUB * 2].rearrange("p (c f) -> p c f", f=SUB * 2)
        norm_mid = arena_rows[0:XP, 0:XN * D].rearrange("p (j d) -> p j d", d=D)
        xb = arena_rows[:, 0:NBLK * D].rearrange("p (b d) -> p b d", d=D)
        PW = (NBLK * H3W + 1) // 2
        parts1 = arena_rows[:, NBLK * D:NBLK * D + PW].bitcast(bf16)[:, 0:NBLK * H3W].rearrange(
            "p (b c) -> p b c", c=H3W)
        sums_st = acc[:, 1, 0:NBUF * 512].rearrange("p (n c) -> p n c", n=NBUF)
        hid_t = acc[0:HID, 1, NBUF * 512:(NBUF + 1) * 512]
        hid_at = (NBUF + 1) * 512
        hid_c, rest_c = (acc[:, 1, hid_at + n * 4 * HID:hid_at + (n + 1) * 4 * HID].rearrange(
            "p (q c) -> p q c", c=HID) for n in range(2))
        parts_at = hid_at + 8 * HID
        early_ld = acc[:, 1, parts_at + PW:parts_at + PW + NBUF * 512].rearrange("p (n c) -> p n c", n=NBUF)
        parts2 = acc[:, 1, parts_at:parts_at + PW].bitcast(bf16)[:, 0:NBLK * H3W].rearrange(
            "p (b c) -> p b c", c=H3W)
        node_rows_a = sb("node_rows_a", [P, XN, D], f32)
        xa = node_rows_a[0:XP, :, :]
        g_rows = node_rows_a[:, 0:NBLK, :]
        NT = FULL_T + 1
        tile_rows = node_rows_a[0:1, :, :].rearrange("p j d -> p (j d)")[:, 0:2 * NT].rearrange(
            "p (k t) -> p k t", k=2)
        xc = sb("xc", [P, XN, D], f32)
        right1 = xc[:, 0:NBLK, 0:HID]
        centred = edge_rows_f[:, :, :, :].rearrange("p a b e -> p (a b e)")[:, 0:NBLK * D].rearrange(
            "p (b d) -> p b d", d=D)
        blk_used = [NBLK * HDST // 2]

        def in_edge_rows(n):
            blk_used[0] += n
            assert blk_used[0] <= 2 * BLK * SUB
            return edge_rows_f[:, :, :, :].rearrange("p a b e -> p (a b e)")[:, blk_used[0] - n:blk_used[0]]

        blk_x = in_edge_rows(2 * D).rearrange("p (j d) -> p j d", j=2)
        blk_sum = in_edge_rows(4 * P).rearrange("p (j h n) -> p j h n", j=2, h=2)
        blk_rows = in_edge_rows(2 * D).rearrange("p (j d) -> p j d", j=2)
        blk_sq = in_edge_rows(D)
        blk_t = in_edge_rows(2 * P)[0:D, :].rearrange("p (j n) -> p j n", j=2)
        blk_g = in_edge_rows(2 * (HID + 1)).rearrange("p (j d) -> p j d", j=2)
        early_st = in_edge_rows(2 * HDST).rearrange("p (h d) -> p h d", h=2)
        blk_stat = sb("blk_stat", [P, 2, 4], f32)
        eps = sb("eps", [P, 1], f32)
        nodes_i = sb("nodes_i", [1, STEPS - 2], i32)
        stat = sb("stat", [P, 4, XN], f32)
        recip_cnt = sb("recip_cnt", [P, NBLK], f32)
        basis_sb = sb("basis_sb", [P, 2, D], f32)
        w1_sb = sb("w1_sb", [D, 2 * HID], f32)
        w2l_sb = sb("w2l_sb", [H3W, D], f32)
        w2r_sb = sb("w2r_sb", [HID, D], f32)
        bias_bc = sb("bias_bc", [P, D], f32)
        b1_bc = sb("b1_bc", [P, HID], f32)
        b2_bc = sb("b2_bc", [P, D], f32)

        ps = ctx.enter_context(nc.psum_tensor("ps", [P, 8, 512], f32))

        blk_banks = [(ps[:, 6, :], ps[:, 7, :]), (ps[:, 0, :], ps[:, 1, :])]

        early_ps = ps[0:H3W, 7, 0:HDST]

        s_pad = sem("s_pad")
        s_dst = sem("s_dst")
        s_src = sem("s_src")
        s_wgt = sem("s_wgt")
        s_xa = sem("s_xa")
        s_comp = sem("s_comp")
        s_consts = sem("s_consts")
        types_stored = sem("types_stored")
        types_loaded = sem("types_loaded")
        pool_consts = sem("pool_consts")
        dve_step = sem("dve_step")
        from_parts_step = sem("from_parts_step")
        rows_cast = sem("rows_cast")
        keys_ready = sem("keys_ready")
        keys_stored = sem("keys_stored")
        low_high_ready = sem("low_high_ready")
        low_high_tr = sem("low_high_tr")
        tiles_ready = sem("tiles_ready")
        tiles_stored = sem("tiles_stored")
        tile_high_back = sem("tile_high_back")
        tile_rows_back = sem("tile_rows_back")
        meta_ready = sem("meta_ready")
        meta_stored = sem("meta_stored")
        meta_back = sem("meta_back")
        thr_ready = sem("thr_ready")
        tile_signs = sem("tile_signs")
        tile_cnt_ready = sem("tile_cnt_ready")
        key_rows_in = sem("key_rows_in")
        starts_ready = sem("starts_ready")
        starts_stored = sem("starts_stored")
        starts_back = sem("starts_back")
        tr_done = sem("tr_done")
        dst_copied = sem("dst_copied")
        cols_copied = sem("cols_copied")
        comp_ready = sem("comp_ready")
        types_hot_ready = sem("types_hot_ready")
        coef_mm = sem("coef_mm")
        coef_done = sem("coef_done")
        var_ready = sem("var_ready")
        std_ready = sem("std_ready")
        table_rows_ready = sem("table_rows_ready")
        table_stored = sem("table_stored")
        idx_ready = sem("idx_ready")
        idx_ready_sage = sem("idx_ready_sage")
        gathers_begun = sem("gathers_begun")
        gathered = [sem(f"gathered{u}") for u in range(U)]
        onehot_ready = sem("onehot_ready")
        wts_ready = sem("wts_ready")
        mm_done = sem("mm_done")
        psum_free = sem("psum_free")
        stand_in = sem("stand_in")
        x_step = sem("x_step")
        x_wts_ready = sem("x_wts_ready")
        x_mm_done = sem("x_mm_done")
        sums_ready = sem("sums_ready")
        keys_loaded = [sem(f"keys_loaded{n}") for n in range(WPS)]
        key_rel_ready = sem("key_rel_ready")
        hots_ready = sem("hots_ready")
        win_mm = sem("win_mm")
        win_read = sem("win_read")
        copies_begun = sem("copies_begun")
        pe_waited = sem("pe_waited")
        a_stored = [sem(f"a_stored{h}") for h in range(2)]
        s_xb = sem("s_xb")
        x_loaded = [sem(f"x_loaded{j}") for j in range(2)]
        blk_step = [sem(f"blk_step{j}") for j in range(2)]
        blk_zeroed = sem("blk_zeroed")
        blk_summed = sem("blk_summed")
        blk_mm = sem("blk_mm")
        blk_x_ready = sem("blk_x_ready")
        blk_act = sem("blk_act")
        blk_std = sem("blk_std")
        blk_normed = sem("blk_normed")
        blk_tr = sem("blk_tr")
        blk_t_ready = sem("blk_t_ready")
        blk_w1_mm = sem("blk_w1_mm")
        faults_mm = sem("faults_mm")
        faults_in = sem("faults_in")
        fault_known = sem("fault_known")
        a_loaded = [sem(f"a_loaded{b}") for b in range(NBUF)]
        parts_ready = sem("parts_ready")
        early_mm = sem("early_mm")
        early_read = sem("early_read")
        early_stored = [sem(f"early_stored{h}") for h in range(2)]
        early_loaded = [sem(f"early_loaded{n}") for n in range(NBUF)]
        chunk_step = sem("chunk_step")
        recip_begun = sem("recip_begun")
        sums_mm = sem("sums_mm")
        hid_ready = sem("hid_ready")
        hid_tr = sem("hid_tr")
        hid_t_ready = sem("hid_t_ready")
        root_mm = sem("root_mm")
        parts2_ready = sem("parts2_ready")
        out_mm = sem("out_mm")
        out_step = sem("out_step")
        out_ready = sem("out_ready")
        general_step = sem("general_step")
        conv_mm = sem("conv_mm")
        conv_read = sem("conv_read")
        node_mm = sem("node_mm")
        node_in = sem("node_in")
        ps_read = sem("ps_read")
        s_out = sem("s_out")

        block = ctx.enter_context(nc.Block())

        def node_rows(dram, first, last):
            return dram[first * P:last * P, :].rearrange("(b p) d -> p b d", p=P)

        a_buf = [arena[:, 0:a_words].bitcast(f8).rearrange("p (h n) -> p h n", h=CH)
                 for arena in (arena_coef, arena_cols, acc[:, 0, :])]
        BUF2 = [(FULLC - n) % NBUF for n in range(NBUF)]
        POOL_CONSTS = 17

        def late_from(c):
            return max(4 * c - 2, 0)

        CONST_DMAS = 16 * (NB + 6 + 3)

        @block.sync
        def _(sp):
            sp.wait_ge(s_pad, 3)
            full = FULL_T // P
            for dram, tile, s in ((dst, dst_rows, s_dst), (src, src_rows, s_src), (weight_e, wgt_rows, s_wgt)):
                sp.dma_start(tile[:, 0:full, :],
                             dram[0:full * P * SUB].rearrange("(b p e) -> p b e", p=P, e=SUB)).then_inc(s, 16)
                left = FULL_T - full * P
                sp.dma_start(tile[0:left, full, :],
                             dram[full * P * SUB:FULL_T * SUB].rearrange("(p e) -> p e", e=SUB)).then_inc(s, 16)
                sp.dma_start(tile[left:left + 1, full, 0:REST],
                             dram[FULL_T * SUB:E].rearrange("(p e) -> p e", p=1)).then_inc(s, 16)
            sp.dma_start(types_dram[0:E].rearrange("(a b) -> a b", a=16),
                         etype.rearrange("(a b) -> a b", a=16)).then_inc(types_stored, 16)
            sp.wait_ge(pool_consts, POOL_CONSTS)
            sp.dma_start(types_dram[E:(STEPS + 2) * ST * SUB].rearrange("(a b) -> a b", a=64),
                         no_type[:, :]).then_inc(types_stored, 16)
            def load_types(first_tile):
                rows_t = types_dram[bass.ds(first_tile * SUB, ST * SUB)].rearrange(
                    "(a g t e) -> a t g e", a=1, t=TPG, e=SUB)
                for t in range(TPG):
                    sp.dma_start(types[t * NR:(t + 1) * NR, :].rearrange("p (g e) -> p g e", e=SUB),
                                 rows_t[:, t, :, :].to_broadcast([NR, U, SUB])).then_inc(types_loaded, 16)

            sp.wait_ge(types_stored, 32)
            load_types(0)
            sp.wait_ge(tiles_ready, 1)
            for k in range(2):
                sp.dma_start(tiles_dram[k, :].rearrange("(b t) -> b t", t=P), tiles_t[:, k, :]).then_inc(tiles_stored, 16)
            sp.wait_ge(tiles_stored, 32)
            sp.dma_start(tile_high, tiles_dram[1:2, :].to_broadcast([P, TALL])).then_inc(tile_high_back, 16)
            sp.wait_ge(keys_ready, 1)
            sp.dma_start(keys_dram.rearrange("(b p) f -> p b f", p=P),
                         keys_all.rearrange("p b e k -> p b (e k)")).then_inc(keys_stored, 16)
            sp.wait_ge(meta_ready, 1)
            for k in range(2):
                sp.dma_start(meta_dram[k, :].rearrange("(b g) -> b g", g=GB), meta_t[:, k, :]).then_inc(meta_stored, 16)
            sp.wait_ge(meta_stored, 32)
            sp.dma_start(meta[0:1, :, :], meta_dram.rearrange("(p k) g -> p k g", p=1)).then_inc(meta_back, 16)
            sp.dma_start(base_bc[:, :], meta_dram[0:1, :].to_broadcast([P, GALL])).then_inc(meta_back, 16)
            sp.wait_ge(table_rows_ready, 1)
            sp.dma_start(tile_rows, tiles_dram[:, 0:NT].rearrange("(p k) t -> p k t", p=1)).then_inc(tile_rows_back, 16)
            sp.wait_ge(starts_ready, 1)
            sp.dma_start(start_dram.rearrange("(p c) -> p c", c=WC), start_i[0:WP, :]).then_inc(starts_stored, 16)
            sp.wait_ge(starts_stored, 16)
            sp.dma_start(starts, start_dram.rearrange("(p w) -> p w", p=1)).then_inc(starts_back, 16)
            sp.wait_ge(types_hot_ready, 1)
            load_types(ST)
            for h in range(2):
                sp.dma_start(a_dram[HALVES + 1 + h, :, :],
                             a_half[:, h, :, :].rearrange("p b d -> p (b d)").bitcast(bf16)).then_inc(a_stored[h], 16)
                sp.dma_start(early_dram[HALVES + 2 + h, :, :], early_st[0:H3W, h, :]).then_inc(early_stored[h], 16)
            sp.wait_ge(blk_zeroed, 1)
            sp.dma_start(blk_x[:, 0, :], x[0:P, :]).then_inc(x_loaded[0], 16)
            sp.dma_start(blk_x[0:NREST, 1, :], x[(NBLK - 1) * P:N, :]).then_inc(x_loaded[1], 16)
            sp.wait_ge(starts_back, 16)
            blk = sp.alloc_register("sp_blk")
            sp.reg_mov(blk, 0)

            keys_flat = keys_dram.rearrange("t f -> (t f)")
            regs = [sp.alloc_register(f"sp_start{n}") for n in range(WPS)]

            def load_keys(it, s):
                sp.wait_ge(hots_ready, it * WPS + (s + 1))
                first = sp.snap(regs[s], min_val=0, max_val=FULL_T * SUB + SUB)
                sp.dma_start(keys[:, s, :, :],
                             keys_flat[bass.ds(first * 2, P * WVIS * 2)].rearrange("(p v k) -> p v k", v=WVIS, k=2)
                             ).then_inc(keys_loaded[s], 16)

            def store_half(index, h):
                sp.dma_start(a_dram[bass.ds(index, 1), :, :].rearrange("a p n -> p (a n)"),
                             a_half[:, h, :, :].rearrange("p b d -> p (b d)").bitcast(bf16)).then_inc(a_stored[h], 16)

            def store_early(index, h):
                sp.dma_start(early_dram[bass.ds(index, 1), :, :].rearrange("a p n -> p (a n)"),
                             early_st[0:H3W, h, :]).then_inc(early_stored[h], 16)

            with sp.Fori(0, STEPS) as it:
                sp.load(regs, starts[:, bass.ds(it * WPS, WPS)])
                for s in range(HW):
                    load_keys(it, s)
                sp.wait_ge(win_read, it * WPS + 2)
                store_half(it * 2, 1)
                sp.wait_ge(early_read, it * 2 + 1)
                store_early(it * 2, 0)
                for s in range(HW, WPS):
                    load_keys(it, s)
                sp.wait_ge(types_hot_ready, it + 2)
                load_types((it + 2) * ST)
                sp.wait_ge(win_read, it * WPS + (HW + 2))
                store_half(it * 2 + 1, 0)
                sp.wait_ge(blk_x_ready, it + 1)
                row = sp.snap(blk, min_val=0, max_val=NBLK - 2)
                sp.dma_start(blk_x[:, 0, :], x[bass.ds(row * P, P), :]).then_inc(x_loaded[0], 16)
                sp.reg_mov(blk, it)
                sp.wait_ge(early_read, it * 2 + 2)
                store_early(it * 2 + 1, 1)
            sp.wait_ge(win_read, STEPS * WPS + 2)
            store_half(HALVES, 1)
            sp.wait_ge(early_read, STEPS * 2 + 1)
            store_early(HALVES, 0)

            def load_matrix(chunk, buf, halves=CH, first=0):
                src_cols_ = slice(first * HDST // 2, NBLK * HDST // 2)
                sp.dma_start(a_buf[buf][:, 0:halves, :].bitcast(bf16)[:, :, src_cols_],
                             a_dram[bass.ds(chunk * CH + 1, halves), :, src_cols_].rearrange("h p n -> p h n")
                             ).then_inc(a_loaded[buf], 16)

            for h in range(2):
                sp.wait_ge(a_stored[h], 16 * (STEPS + 1 + h))
                sp.wait_ge(early_stored[h], 16 * (STEPS + 2 - h))
            sp.wait_ge(coef_done, STEPS + 1)
            sp.wait_ge(mm_done, GROUPS + U)
            load_matrix(FULLC, 0, RESTH)
            sp.wait_ge(fault_known, 1)
            fault = sp.value_load(fault_i[0:1, 0:1], min_val=0, max_val=1)
            with sp.If(fault < 1):
                sp.wait_ge(idx_ready, GROUPS + U)
                for e in range(1, FULLC + 1):
                    c = FULLC - e
                    if e == 2:
                        sp.wait_ge(blk_summed, STEPS + 2)
                    if e >= NBUF:
                        sp.wait_ge(conv_mm, e - NBUF + 1)
                    load_matrix(c, e % NBUF, first=late_from(c) if c >= NBUF else 0)
                    if c:
                        if e == 1:
                            sp.wait_ge(blk_summed, STEPS + 2)
                        if e > NBUF:
                            sp.wait_ge(sums_mm, e - NBUF + 1)
                        sp.dma_start(early_ld[0:H3W, e % NBUF, :].rearrange("p (h d) -> p h d", d=HDST),
                                     early_dram[c * CH + 2:(c + 1) * CH + 2, :, :].rearrange("h p d -> p h d")
                                     ).then_inc(early_loaded[e % NBUF], 16)
                with sp.Fori(0, TRIPS - 1) as it:
                    for n in range(NBUF):
                        sp.wait_ge(conv_mm, it * NBUF + (FULLC + 2 + n))
                        load_matrix(it * NBUF + (NBUF + n), BUF2[n])
                sp.wait_ge(conv_mm, FULLC + 2 + NBUF * (TRIPS - 1))
                load_matrix(FULLC, 0, RESTH)
            with sp.Else():
                sp.wait_ge(a_loaded[0], 16)
                sp.dma_start(xb[:, 0:NBLK - 1, :], node_rows(x, 0, NBLK - 1)).then_inc(s_xb, 16)
                sp.dma_start(xb[0:NREST, NBLK - 1, :], x[(NBLK - 1) * P:N, :]).then_inc(s_xb, 16)
            sp.nop()

        @block.gpsimd
        def _(pool):
            pool.memset(no_type[:, :], -1).then_inc(pool_consts, 1)
            pool.memset(neg_exact[:, :], -float(EXACT)).then_inc(pool_consts, 1)
            pool.memset(ones[:, :], 1.0).then_inc(pool_consts, 1)
            pool.memset(eps[:, :], EPS).then_inc(pool_consts, 1)
            pool.iota(nodes_i[:, :], [[P, STEPS - 2]], base=P, channel_multiplier=0).then_inc(pool_consts, 1)
            pool.iota(iota_i[:, :], [[1, WIN]], base=0, channel_multiplier=0).then_inc(pool_consts, 1)
            pool.iota(rel_i[:, :], [[0, 1]], base=0, channel_multiplier=1).then_inc(pool_consts, 1)
            pool.iota(shift_i[:, :], [[-WIN, XMAX]], base=-WIN, channel_multiplier=0).then_inc(pool_consts, 1)
            pool.iota(thr_i[:, :], [[WD, WC]], base=0, channel_multiplier=WD * WC).then_inc(pool_consts, 1)
            pool.iota(wbase_i[:, :], [[WCOL, NW]], base=0, channel_multiplier=0).then_inc(pool_consts, 1)
            pool.iota(iota_w_i[:, :], [[1, WCOL]], base=0, channel_multiplier=0).then_inc(pool_consts, 1)
            pool.memset(ident[:, :], 0.0).then_inc(pool_consts, 1)
            pool.memset(from_parts[:, :], 0.0).then_inc(pool_consts, 1)
            pool.wait_ge(pool_consts, 13)
            pool.affine_select(out=ident[:, :], in_=ident[:, :], compare_op=ALU.not_equal, fill=1.0, base=0,
                               pattern=[[-1, P]], channel_multiplier=1).then_inc(pool_consts, 1)
            for n, (base, wide) in enumerate(((0, HID + 1), (-(HID + 1), HID), (-(2 * HID + 1), HID))):
                if n:
                    pool.wait_ge(from_parts_step, n)
                ins = pool.affine_select(out=from_parts[:, 0:wide], in_=from_parts[:, 0:wide],
                                         compare_op=ALU.not_equal, fill=1.0, base=base,
                                         pattern=[[-1, wide]], channel_multiplier=1)
                ins.then_inc(from_parts_step if n < 2 else pool_consts, 1)
            pool.memset(faults[:, :], 0.0).then_inc(pool_consts, 1)
            pool.memset(acc[:, 1, :], 0.0).then_inc(pool_consts, 1)
            pool.wait_ge(tile_cnt_ready, 1)
            pool.wait_ge(keys_stored, 16)
            for c in range(WC):
                pool.indirect_dma_start(
                    key_rows[:, c, :], None, keys_dram,
                    bass.IndirectOffsetOnAxis(ap=tile_cnt_i[0:WP, c:c + 1].bitcast(u32), axis=0),
                ).then_inc(key_rows_in, 16)
            pool.wait_ge(table_stored, 16)
            pool.wait_ge(tiles_stored, 32)

            def gather_group(k, ready, it, u):
                pool.wait_ge(ready, it * U + (GROUPS * max(k - 1, 0) + u + 1))
                pool.wait_ge(mm_done, it * U + (GROUPS * k + u + 1))
                pool.sem_inc(gathers_begun, 1)
                for t in range(TPG):
                    pool.indirect_dma_start(
                        rows[:, u, t, :], None, tables[k],
                        bass.IndirectOffsetOnAxis(ap=idx[:, u, t:t + 1].bitcast(u32), axis=0),
                    ).then_inc(gathered[u], 16)

            def gathers(k, ready):
                with pool.Fori(0, STEPS) as it:
                    for u in range(U):
                        gather_group(k, ready, it, u)

            gathers(0, idx_ready)
            pool.wait_ge(fault_known, 1)
            fault = pool.value_load(fault_i[0:1, 0:1], min_val=0, max_val=1)
            with pool.If(fault > 0):
                for k in (1, 2):
                    pool.wait_ge(table_stored, 32 * k + 16)
                    gathers(k, idx_ready_sage)
            pool.nop()

        @block.scalar
        def _(act):
            act.dma_start(xa, x.rearrange("(p j) d -> p j d", p=XP)).then_inc(s_xa, 16)
            act.wait_ge(s_pad, 4)
            for t in range(TPG):
                act.dma_start(comp_f[t * NR:(t + 1) * NR, t * NB:(t + 1) * NB], w_comp).then_inc(s_comp, 16)
            for b in range(NB):
                act.dma_start(basis_sb[(b // 2) * D:(b // 2 + 1) * D, b % 2, :], w_basis[b, :, :]).then_inc(s_consts, 16)
            act.dma_start(w1_sb[:, 0:HID], w1_l).then_inc(s_consts, 16)
            act.dma_start(w1_sb[:, HID:2 * HID], w1_r).then_inc(s_consts, 16)
            for first in (0, HID + 1, 2 * HID + 1):
                act.dma_start(w2l_sb[first:first + HID, :], w2_l).then_inc(s_consts, 16)
            act.dma_start(w2r_sb[:, :], w2_r).then_inc(s_consts, 16)
            for vec, tile, n in ((bias, bias_bc, D), (b1, b1_bc, HID), (b2, b2_bc, D)):
                act.dma_start(tile[:, :], vec.rearrange("(a n) -> a n", a=1).to_broadcast([P, n])).then_inc(s_consts, 16)
            act.sem_inc(win_read, 2)
            act.sem_inc(conv_read, NBUF)
            act.sem_inc(early_read, 1)
            for n in range(8):
                tile = src_cols if n < 4 else wgt_cols
                q, w = (n % 4) * 512, min(512, TALL - (n % 4) * 512)
                act.wait_ge(tr_done, n + 1)
                act.activation(tile[:, q:q + w], ps[:, n % 6, 0:w], ACT.Copy).then_inc(cols_copied, 1)
            act.wait_ge(cols_copied, 8)

            def copy_idx(tile0, u, ready):
                act.activation(idx[:, u, :], src_cols[:, bass.ds(tile0, TPG)], ACT.Copy).then_inc(ready, 1)

            for u in range(U):
                copy_idx(u * TPG, u, idx_ready)
            act.wait_ge(thr_ready, 1)
            act.wait_ge(tile_high_back, 16)
            for c in range(WC):
                if c == WC - 2:
                    act.wait_ge(var_ready, 1)
                    act.activation(stat[0:XP, 3, :], stat[0:XP, 2, :], ACT.Sqrt).then_inc(std_ready, 1)
                if c:
                    act.wait_ge(tile_signs, c)
                act.activation(scratch, tile_high, ACT.Sign, bias=thr[:, 2, c:c + 1], scale=-1.0,
                               accum_out=tile_cnt[:, c:c + 1]).then_inc(tile_signs, 1)
            act.wait_ge(table_rows_ready, 1)
            act.dma_start(tables[0].rearrange("(p j) d -> p j d", p=XP), xc[0:XP, :, :]).then_inc(table_stored, 16)
            act.wait_ge(pool_consts, POOL_CONSTS)
            act.activation(parts1.rearrange("p b c -> p (b c)"), acc[:, 1, 0:NBLK * H3W], ACT.Copy).then_inc(parts_ready, 1)

            def copy_early(n, it, h):
                act.wait_ge(early_mm, n + 2)
                act.wait_ge(early_stored[h], it * 16 + (16 if h else 32))
                act.sem_inc(copies_begun, 1)
                act.activation(early_st[0:H3W, h, :], early_ps, ACT.Copy).then_inc(early_read, 1)

            def blk_deviation(i, j, b):
                st = blk_stat[:, j, :]
                act.wait_ge(blk_x_ready, i + 1)
                act.sem_inc(copies_begun, 1)
                act.activation(blk_sq[:, :], xb[:, b, :].rearrange("p a d -> p (a d)"), ACT.Copy, scale=-1.0 / D,
                               accum_out=st[:, 0:1]).then_inc(blk_act, 1)
                act.wait_ge(blk_act, i * 2 + 1)
                act.sem_inc(copies_begun, 1)
                act.activation(blk_sq[:, :], xb[:, b, :].rearrange("p a d -> p (a d)"), ACT.Square, bias=st[:, 0:1],
                               accum_out=st[:, 1:2]).then_inc(blk_act, 1)
                act.wait_ge(blk_act, i * 2 + 2)
                act.activation(st[:, 2:3], st[:, 1:2], ACT.Sqrt, bias=eps[:, 0:1], scale=1.0 / D).then_inc(blk_std, 1)

            def blk_transposed(i, j):
                act.wait_ge(blk_tr, i + 1)
                act.activation(blk_t[:, j, :], blk_banks[j][1][0:D, 0:P], ACT.Copy).then_inc(blk_t_ready, 1)

            blk = act.alloc_register("act_blk")
            blk_next = act.alloc_register("act_blk_next")
            act.reg_mov(blk, 0)
            act.reg_mov(blk_next, 0)
            with act.Fori(0, STEPS) as it:
                for u in range(U):
                    if u == 2:
                        copy_early(it * 2, it, 1)
                    if u == 6:
                        copy_early(it * 2 + 1, it, 0)
                    if u == 2:
                        blk_deviation(it, 0, bass.ds(act.snap(blk, min_val=0, max_val=NBLK - 2), 1))
                    if u == 4:
                        blk_transposed(it, 0)
                    for j in range(2):
                        s = 2 * u + j
                        act.wait_ge(win_mm, it * WPS + (s + 3))
                        if s == 0:
                            act.wait_ge(early_mm, it * 2 + 1)
                        if s == HW:
                            act.wait_ge(early_mm, it * 2 + 2)
                        if s % HW == 0:
                            act.wait_ge(a_stored[s // HW], it * 16 + 16)
                        act.sem_inc(copies_begun, 1)
                        win = ps[:, 3 + j, 0:WCOL]
                        act.activation(a_half[:, s // HW, :, (s % HW) * WD:(s % HW + 1) * WD].rearrange("p b d -> p d b"),
                                       win.rearrange("p (d b) -> p d b", b=NBLK), ACT.Copy, saturate=True)
                        act.wait_ge(win_read, it * WPS + (s + 2))
                        act.activation(above[:, :], win, ACT.Relu, bias=neg_exact[:, 0:1],
                                       accum_out=above_sum[:, bass.ds(it * WPS + s, 1)]).then_inc(win_read, 1)
                    act.wait_ge(mm_done, it * U + (U + u + 1))
                    copy_idx((it + 1) * ST + u * TPG, u, idx_ready)
                act.reg_mov(blk, blk_next)
                act.reg_mov(blk_next, it)
            for j in range(2):
                blk_deviation(STEPS + j, j, slice(NBLK - 2 + j, NBLK - 1 + j))
            for j in range(2):
                blk_transposed(STEPS + j, j)
            act.wait_ge(fault_known, 1)
            fault = act.value_load(fault_i[0:1, 0:1], min_val=0, max_val=1)

            def copy_sums(n, bank, stage, wide):
                act.wait_ge(conv_mm, n)
                act.activation(sums_st[0:H3W, stage, 0:wide], ps[0:H3W, bank, 0:wide], ACT.Copy).then_inc(conv_read, 1)

            def copy_hidden(n, wide):
                act.wait_ge(hid_tr, n)
                act.activation(hid_t[:, 0:wide], ps[0:HID, 5, 0:wide], ACT.Copy).then_inc(hid_t_ready, 1)

            with act.If(fault < 1):
                copy_sums(1, NBUF, 0, RESTH * HDST)
                copy_hidden(1, RESTH * HDST)
                with act.Fori(0, TRIPS) as it:
                    for n in range(NBUF):
                        copy_sums(it * NBUF + (n + 2), n, n, 512)
                        copy_hidden(it * NBUF + (n + 2), 512)
                with act.Fori(0, TRIPS) as it:
                    for n in range(NBUF):
                        copy_sums(it * NBUF + (FULLC + 2 + n), n, n, 512)
                        act.wait_ge(out_ready, it * NBUF + (n + 1))
                        act.sem_inc(copies_begun, 1)
                        blk0 = it * (NBUF * 4) + n * 4
                        act.dma_start(out[bass.ds(blk0 * P, 4 * P), :].rearrange("(b p) d -> p b d", p=P),
                                      g_rows[:, bass.ds(blk0, 4), :]).then_inc(s_out, 16)
                copy_sums(2 * FULLC + 2, NBUF, 0, RESTH * HDST)
                act.wait_ge(out_ready, FULLC + 1)
                act.dma_start(out[(NBLK - 1) * P:N, :], g_rows[0:NREST, NBLK - 1, :]).then_inc(s_out, 16)
                act.wait_ge(s_out, 16 * (FULLC + 1))
            with act.Else():
                act.wait_ge(var_ready, 2)
                act.activation(stat[:, 3, 0:NBLK], stat[:, 2, 0:NBLK], ACT.Sqrt).then_inc(std_ready, 1)
                for k in (1, 2):
                    act.wait_ge(table_rows_ready, k + 1)
                    act.dma_start(node_rows(tables[k], 0, NBLK - 1), g_rows[:, 0:NBLK - 1, :]).then_inc(table_stored, 16)
                    act.dma_start(tables[k][(NBLK - 1) * P:N, :], g_rows[0:NREST, NBLK - 1, :]).then_inc(table_stored, 16)
                    with act.Fori(0, STEPS) as it:
                        for u in range(U):
                            act.wait_ge(mm_done, it * U + (GROUPS * k + u + 1))
                            copy_idx(it * ST + u * TPG, u, idx_ready_sage)
                act.wait_ge(table_rows_ready, 4)
                act.dma_start(node_rows(out, 0, NBLK - 1), g_rows[:, 0:NBLK - 1, :]).then_inc(s_out, 16)
                act.dma_start(out[(NBLK - 1) * P:N, :], g_rows[0:NREST, NBLK - 1, :]).then_inc(s_out, 16)
                act.wait_ge(s_out, 32)
            act.nop()

        @block.vector
        def _(dve):
            def chain(step, base=0):
                done = [0]

                def link(ins):
                    done[0] += 1
                    ins.then_inc(step, 1)
                    dve.wait_ge(step, base + done[0])
                return link

            link = chain(dve_step)
            dve.memset(dst_rows[:, BLK - 1, :], PAD).then_inc(s_pad, 1)
            dve.memset(src_rows[:, BLK - 1, :], 0).then_inc(s_pad, 1)
            dve.memset(wgt_rows[:, BLK - 1, :], 0.0).then_inc(s_pad, 1)
            dve.memset(w2l_sb[:, :], 0.0)
            link(dve.memset(comp_f[:, :], 0.0))
            dve.nop().then_inc(s_pad, 1)
            dve.sem_inc(hots_ready, WPS)
            dve.memset(acc[:, 0, :], 0.0)

            def norm(rows_in, mid, res, p, n, waits, link):
                st = stat[0:p, :, 0:n]
                link(dve.tensor_reduce(st[:, 0, :], rows_in, axis=AX, op=ALU.add))
                link(dve.tensor_scalar(st[:, 0, :], st[:, 0, :], 1.0 / D, None, ALU.mult))
                mean = st[:, 0, :].unsqueeze(2).to_broadcast([p, n, D])
                link(dve.tensor_tensor(mid, rows_in, mean, ALU.subtract))
                link(dve.tensor_tensor(res, mid, mid, ALU.mult))
                link(dve.tensor_reduce(st[:, 1, :], res, axis=AX, op=ALU.add))
                dve.tensor_scalar(st[:, 2, :], st[:, 1, :], 1.0 / D, EPS, ALU.mult, ALU.add).then_inc(var_ready, 1)
                dve.wait_ge(std_ready, waits)
                link(dve.reciprocal(st[:, 1, :], st[:, 3, :]))
                scale = st[:, 1, :].unsqueeze(2).to_broadcast([p, n, D])
                return dve.scalar_tensor_tensor(out=res, in0=mid, scalar=0.0, in1=scale, op0=ALU.max, op1=ALU.mult)

            dve.wait_ge(s_dst, 48)
            link(dve.tensor_copy(dst_rows_f, dst_rows))
            dve.tensor_reduce(low_high[:, 0, 0:BLK], dst_rows_f, axis=AX, op=ALU.min)
            dve.tensor_reduce(low_high[:, 1, 0:BLK], dst_rows_f, axis=AX, op=ALU.max)
            last = dst_rows_f[:, BLK - 1, :]
            fill_off = scratch[:, 0:SUB]
            link(dve.tensor_scalar(fill_off, last, float(PAD), -10.0 * PAD, ALU.is_ge, ALU.mult))
            link(dve.tensor_tensor(fill_off, fill_off, last, ALU.add))
            link(dve.tensor_copy(low_high[:, 2, 0:BLK], low_high[:, 1, 0:BLK]))
            link(dve.tensor_reduce(low_high[:, 2, BLK - 1:BLK], fill_off, axis=AX, op=ALU.max))
            dve.nop().then_inc(low_high_ready, 1)
            dve.wait_ge(s_src, 48)
            blk_of = blk_of_i.rearrange("p (b e) -> p b e", e=SUB)
            dve.tensor_copy(src_rows_f, src_rows)
            link(dve.tensor_single_scalar(blk_of, src_rows, 7, ALU.logical_shift_right))
            dve.nop().then_inc(rows_cast, 1)
            dve.scalar_tensor_tensor(out=keys_all[:, :, :, 0], in0=dst_rows_f, scalar=float(NBLK), in1=blk_of,
                                     op0=ALU.mult, op1=ALU.add)
            link(dve.scalar_tensor_tensor(out=keys_all[:, :, :, 1], in0=blk_of, scalar=-float(P), in1=src_rows_f,
                                          op0=ALU.mult, op1=ALU.add))
            dve.nop().then_inc(keys_ready, 1)
            dve.wait_ge(low_high_tr, 1)
            tr = ps[0:BLK, 6, 0:3 * P].rearrange("b (k n) -> b k n", k=3)
            link(dve.tensor_copy(tiles_t[:, :, :], tr[:, 0:2, :]))
            dve.nop().then_inc(tiles_ready, 1)
            by_group = tr.rearrange("b k (g t) -> b k g t", t=TPG)
            dve.tensor_reduce(low_high_t[:, 0, :], by_group[:, 0, :, :], axis=AX, op=ALU.min)
            link(dve.tensor_reduce(low_high_t[:, 1, :], by_group[:, 2, :, :], axis=AX, op=ALU.max))
            link(dve.tensor_scalar(low_high_t[:, 0, :], low_high_t[:, 0, :], float(N - 1), None, ALU.min))
            link(dve.tensor_tensor(low_high_t[:, 1, :], low_high_t[:, 1, :], low_high_t[:, 0, :], ALU.subtract))
            link(dve.tensor_scalar(low_high_t[:, 1, :], low_high_t[:, 1, :], 0.0, -(WIN - 1) / 2, ALU.max, ALU.add))
            link(dve.tensor_scalar(low_high_t[:, 1, :], low_high_t[:, 1, :], 1.0 / WIN, None, ALU.mult))
            link(dve.tensor_copy(meta_t[:, :, :], low_high_t[:, :, :]))
            dve.nop().then_inc(meta_ready, 1)

            dve.wait_ge(pool_consts, POOL_CONSTS)
            link(dve.tensor_copy(thr[:, 0, :], thr_i[:, :]))
            dve.tensor_scalar(thr[:, 1, :], thr[:, 0, :], float(NBLK), None, ALU.mult)
            link(dve.tensor_scalar(thr[:, 2, :], thr[:, 0, :], -0.5, None, ALU.add))
            dve.nop().then_inc(thr_ready, 1)

            dve.wait_ge(s_xa, 16)
            link(norm(xa, norm_mid, xc[0:XP, :, :], XP, XN, 1, link))
            dve.nop().then_inc(table_rows_ready, 1)

            dve.wait_ge(tile_signs, WC)
            link(dve.tensor_scalar(tile_cnt[:, :], tile_cnt[:, :], 0.5, TALL / 2, ALU.mult, ALU.add))
            link(dve.tensor_copy(tile_cnt_i[:, :], tile_cnt[:, :]))
            dve.nop().then_inc(tile_cnt_ready, 1)
            dve.tensor_copy(iota[:, :], iota_i[:, :])
            dve.tensor_copy(shift[:, :], shift_i[:, :])
            dve.tensor_copy(wbase[:, :], wbase_i[:, :])
            dve.tensor_copy(iota_l[:, :], iota_w_i[:, 0:P])
            dve.tensor_copy(iota_q[:, :], iota_w_i[:, :])
            link(dve.tensor_single_scalar(rel_i[:, :], rel_i[:, :], NR - 1, ALU.bitwise_and))
            link(dve.tensor_copy(rel_of_p[:, :], rel_i[:, :]))
            for n in range(4):
                q, w = n * 512, min(512, TALL - n * 512)
                dve.wait_ge(tr_done, n + 9)
                dve.tensor_copy(dst_rel[:, q:q + w], ps[:, (n + 8) % 6, 0:w]).then_inc(dst_copied, 1)
            dve.wait_ge(dst_copied, 4)
            def count_below(into, a, b, bound, tmp):
                link(dve.tensor_tensor(tmp, a, b, ALU.subtract))
                link(dve.tensor_scalar(tmp, tmp, bound, None, ALU.is_lt, ALU.add, accum_out=into))

            tmp = scratch[:, 0:BLK * (SUB - 1)].rearrange("p (b e) -> p b e", b=BLK)
            count_below(faults[:, 0:1], dst_rows_f[:, :, 1:SUB], dst_rows_f[:, :, 0:SUB - 1], 0.0, tmp)
            dve.wait_ge(tile_rows_back, 16)
            count_below(faults[0:1, 2:3], tile_rows[:, 0, 1:NT], tile_rows[:, 1, 0:NT - 1], 0.0, scratch[0:1, 0:NT - 1])
            dve.wait_ge(meta_back, 32)
            groups_of = dst_rel.rearrange("p (g t) -> p g t", t=TPG)
            link(dve.tensor_tensor(groups_of, groups_of,
                                   base_bc[:, :].unsqueeze(2).to_broadcast([P, GALL, TPG]), ALU.subtract))
            dve.wait_ge(pool_consts, POOL_CONSTS)
            count_below(faults[0:1, 5:6], meta[0:1, 0, 2 * U - 1:(STEPS - 1) * U:U], nodes_i[:, :], 0.0,
                        scratch[0:1, 0:STEPS - 2])
            dve.memset(a_half[:, 1, :, :].rearrange("p b d -> p (b d)").bitcast(bf16), 0.0)
            link(dve.memset(blk_x[:, :, :], 0.0))
            dve.nop().then_inc(blk_zeroed, 1)
            dve.memset(blk_g[:, :, HID:HID + 1], 1.0)
            dve.wait_ge(s_comp, 16 * TPG)
            link(dve.tensor_copy(comp_parts[:, 0, :], comp_f[:, :]))
            link(dve.tensor_tensor(comp_r[:, :], comp_f[:, :], comp_parts[:, 0, :], ALU.subtract))
            link(dve.tensor_copy(comp_parts[:, 1, :], comp_r[:, :]))
            link(dve.tensor_tensor(comp_r[:, :], comp_r[:, :], comp_parts[:, 1, :], ALU.subtract))
            link(dve.tensor_copy(comp_parts[:, 2, :], comp_r[:, :]))
            dve.nop().then_inc(comp_ready, 1)
            dve.wait_ge(key_rows_in, 16 * WC)
            for c in range(WC):
                link(dve.tensor_scalar(scratch[0:WP, 0:SUB], key_rows[:, c, 0:2 * SUB:2], thr[0:WP, 1, c:c + 1], None,
                                       ALU.is_lt, ALU.add, accum_out=edge_cnt[0:WP, c:c + 1]))
            link(dve.scalar_tensor_tensor(out=edge_cnt[0:WP, :], in0=tile_cnt[0:WP, :], scalar=float(SUB),
                                          in1=edge_cnt[0:WP, :], op0=ALU.mult, op1=ALU.add))
            link(dve.tensor_copy(start_i[0:WP, :], edge_cnt[0:WP, :]))
            dve.nop().then_inc(starts_ready, 1)

            dve.wait_ge(starts_back, 16)
            lens = scratch[32:33, 0:NW - 1]
            link(dve.tensor_tensor(lens, starts[:, 1:NW], starts[:, 0:NW - 1], ALU.subtract))
            link(dve.tensor_scalar(lens, lens, float(P * WVIS), None, ALU.is_gt, ALU.add, accum_out=faults[32:33, 3:4]))
            link(dve.tensor_scalar(faults[32:33, 4:5], starts[:, NW - 1:NW], float(E - P * WVIS), None, ALU.is_lt))
            dve.wait_ge(keys_stored, 16)
            dve.wait_ge(table_stored, 16)
            dve.wait_ge(parts_ready, 1)
            dve.wait_ge(s_consts, CONST_DMAS)

            def types_to_hot(n_expr):
                dve.wait_ge(types_loaded, n_expr * (16 * TPG))
                dve.tensor_scalar(types_hot[:, :], types[:, :], rel_of_p[:, 0:1], None,
                                  ALU.is_equal).then_inc(types_hot_ready, 1)

            def coefficients(n_expr, tile0):
                dve.wait_ge(coef_mm, n_expr)
                dve.tensor_tensor(coef[:, bass.ds(tile0, ST), :],
                                  ps[:, 5, 0:ST * NB].rearrange("p (t b) -> p t b", b=NB),
                                  wgt_cols[:, bass.ds(tile0, ST)].unsqueeze(2).to_broadcast([P, ST, NB]),
                                  ALU.mult).then_inc(coef_done, 1)

            dve.wait_ge(cols_copied, 8)
            types_to_hot(1)
            coefficients(1, 0)

            iota_w = iota[:, :].unsqueeze(1).to_broadcast([P, TPG, WIN])

            def weigh(into, hots, cf):
                return dve.tensor_tensor(into, hots.unsqueeze(2).to_broadcast([P, TPG, NB, WIN]),
                                         cf.unsqueeze(3).to_broadcast([P, TPG, NB, WIN]), ALU.mult)

            x_done = dve.alloc_register("dve_x_done")
            x_steps = dve.alloc_register("dve_x_steps")
            x_base = dve.alloc_register("dve_x_base")
            prev = dve.alloc_register("dve_prev_base")
            dve.reg_mov(x_done, 0)
            dve.reg_mov(x_steps, 0)
            regs = [dve.alloc_register(f"dve_meta{n}") for n in range(2 * U)]

            def window_keys(it, u):
                for j in range(2):
                    dve.wait_ge(keys_loaded[2 * u + j], it * 16 + 16)
                dve.tensor_tensor(key_rel[:, u % 2, :, :], keys[:, 2 * u:2 * u + 2, :, 0],
                                  wbase[:, bass.ds(it * WPS + 2 * u, 2)].unsqueeze(2).to_broadcast([P, 2, WVIS]),
                                  ALU.subtract).then_inc(key_rel_ready, 1)

            BLK_STEPS = 7

            def blk_sums(i, j, b, added):
                dve.wait_ge(psum_free, added)
                dve.tensor_copy(blk_sum[:, j, :, :], acc[:, :, b]).then_inc(blk_summed, 1)

            def blk_done(i, j, n):
                return n if j else i * BLK_STEPS + n

            def blk_layer(n, i, j, b):
                if n == 0:
                    dve.wait_ge(blk_mm, i + 1)
                    dve.tensor_tensor(blk_rows[:, j, :], blk_banks[j][0][:, 0:D], bias_bc[:, :],
                                      ALU.add).then_inc(blk_step[j], 1)
                else:
                    dve.wait_ge(x_loaded[j], 16 if j else i * 16 + 16)
                    dve.wait_ge(blk_step[j], blk_done(i, j, 1))
                    dve.scalar_tensor_tensor(out=xb[:, b, :].rearrange("p a d -> p (a d)"), in0=blk_rows[:, j, :],
                                             scalar=0.0, in1=blk_x[:, j, :], op0=ALU.max, op1=ALU.add
                                             ).then_inc(blk_x_ready, 1)

            def blk_norm(i, j, b):
                st = blk_stat[:, j, :]
                dve.wait_ge(blk_std, i + 1)
                dve.reciprocal(st[:, 3:4], st[:, 2:3]).then_inc(blk_step[j], 1)
                dve.tensor_scalar(blk_rows[:, j, :], xb[:, b, :].rearrange("p a d -> p (a d)"), st[:, 0:1], 0.0,
                                  ALU.add, ALU.max).then_inc(blk_normed, 1)

            def blk_split(n, i, j, b):
                rstd, g = blk_stat[:, j, 3:4], blk_g[:, j, 0:HID]
                hi_one, mid_, lo = (parts1[:, b, a:z].rearrange("p a c -> p (a c)")
                                    for a, z in ((0, HID + 1), (HID + 1, 2 * HID + 1), (2 * HID + 1, H3W)))
                left, right = (blk_banks[j][0][:, D + q * HID:D + (q + 1) * HID] for q in range(2))
                if n == 0:
                    dve.wait_ge(blk_w1_mm, i + 1)
                    if j == 0:
                        dve.wait_ge(parts_ready, i + 1)
                dve.wait_ge(blk_step[j], blk_done(i, j, 2 + n))
                if n == 0:
                    dve.scalar_tensor_tensor(out=right1[:, b, :].rearrange("p a c -> p (a c)"), in0=right,
                                             scalar=rstd, in1=b1_bc[:, :], op0=ALU.mult, op1=ALU.add)
                    ins = dve.tensor_scalar(g, left, rstd, None, ALU.mult)
                elif n == 1:
                    ins = dve.tensor_copy(hi_one, blk_g[:, j, :])
                elif n == 2:
                    ins = dve.tensor_tensor(g, g, hi_one[:, 0:HID], ALU.subtract)
                elif n == 3:
                    ins = dve.tensor_copy(mid_, g)
                elif n == 4:
                    ins = dve.tensor_tensor(g, g, mid_, ALU.subtract)
                else:
                    ins = dve.tensor_copy(lo, g)
                ins.then_inc(blk_step[j] if n < 5 else parts_ready, 1)


            blk = dve.alloc_register("dve_blk")
            blk_next = dve.alloc_register("dve_blk_next")
            dve.reg_mov(blk, 0)
            dve.reg_mov(blk_next, 0)

            def window_hots(it, u, j):
                dve.wait_ge(win_mm, it * WPS + (2 * u + j + 1))
                for v in range(WVIS):
                    dve.tensor_scalar(row_hot[:, j, v, :], iota_l[:, :], keys[:, 2 * u + j, v, 1:2], None,
                                      ALU.is_equal)
                if j == 0:
                    dve.wait_ge(key_rel_ready, it * U + (u + 1))
                b = bass.ds(dve.snap(blk, min_val=0, max_val=NBLK - 2), 1)
                for v in range(WVIS):
                    if (u, j) == (1, 1) and v < 2:
                        blk_layer(v, it, 0, b)
                    if (u, j, v) == (3, 1, 1):
                        blk_norm(it, 0, b)
                    if (u, j) == (6, 1):
                        blk_split(v, it, 0, b)
                    if (u, j) == (7, 0):
                        blk_split(3 + v, it, 0, b)
                    ins = dve.tensor_scalar(col_hot[:, j, v, :], iota_q[:, :], key_rel[:, u % 2, j, v:v + 1], None,
                                            ALU.is_equal)
                ins.then_inc(hots_ready, 1)

            def aggregate(k):
                parts, nb = (P, 2) if k == 0 else (D, 1)
                dve.reg_mov(prev, 0)
                dve.memset(ps[:, 1, 0:2 * WIN], 0.0).then_inc(stand_in, 1)
                dve.wait_ge(stand_in, k + 1)
                if k == 0:
                    dve.sem_inc(psum_free, 1)

                def add_sums(slot, base, i_expr):
                    into = acc[0:parts, 0:nb, bass.ds(base, WIN)]
                    dve.wait_ge(mm_done, i_expr + (GROUPS * k + U))
                    dve.wait_ge(psum_free, i_expr + (GROUPS + 1) * k + 1)
                    dve.tensor_tensor(into, into, ps[0:parts, slot, 0:nb * WIN].rearrange("p (b w) -> p b w", w=WIN),
                                      ALU.add).then_inc(psum_free, 1)

                with dve.Fori(0, STEPS) as it:
                    dve.load(regs[0:U], meta[0:1, 0, bass.ds(it * U, U)])
                    dve.load(regs[U:2 * U], meta[0:1, 1, bass.ds(it * U, U)])
                    for u in range(U):
                        i = it * U + u
                        tile0 = it * (U * TPG) + u * TPG
                        extra = dve.snap(regs[U + u], min_val=0, max_val=XMAX - 1)
                        if k == 0 and u == 0:
                            types_to_hot(it + 2)
                        if k == 0 and u == 0:
                            b = dve.snap(blk, min_val=0, max_val=NBLK - 2)
                            blk_sums(it, 0, bass.ds(b * P, P), i + 1)
                        if k == 0:
                            window_keys(it, u)
                        rel = dst_rel[:, bass.ds(tile0, TPG)]
                        cf = coef[:, bass.ds(tile0, TPG), :]
                        dve.tensor_tensor(hot[:, u % 2, :, :], iota_w, rel.unsqueeze(2).to_broadcast([P, TPG, WIN]),
                                          ALU.is_equal).then_inc(onehot_ready if k == 0 else wts_ready, 1)
                        with dve.If(extra > 0):
                            dve.reg_mov(x_base, regs[u])
                            with dve.Fori(0, extra) as j:
                                dve.tensor_scalar(x_rel[:, :], rel, shift[:, bass.ds(j, 1)], None,
                                                  ALU.add).then_inc(x_step, 1)
                                dve.wait_ge(x_step, dve.snap(x_steps) + 1)
                                ins = dve.tensor_tensor(x_hot[:, :, :], iota_w,
                                                        x_rel[:, :].unsqueeze(2).to_broadcast([P, TPG, WIN]),
                                                        ALU.is_equal)
                                if k == 0:
                                    ins.then_inc(x_step, 1)
                                    dve.wait_ge(x_step, dve.snap(x_steps) + 2)
                                    weigh(x_wts[:, :, :, :], x_hot[:, :, :], cf).then_inc(x_wts_ready, 1)
                                else:
                                    ins.then_inc(x_wts_ready, 1)
                                dve.reg_add(x_base, x_base, WIN)
                                into = acc[0:parts, 0:nb,
                                           bass.ds(dve.snap(x_base, min_val=0, max_val=ACCW - WIN), WIN)]
                                dve.wait_ge(x_mm_done, dve.snap(x_done) + 1)
                                dve.wait_ge(psum_free, i + (GROUPS + 1) * k + 1)
                                dve.tensor_tensor(into, into,
                                                  ps[0:parts, 2, 0:nb * WIN].rearrange("p (b w) -> p b w", w=WIN),
                                                  ALU.add).then_inc(x_step, 1)
                                dve.reg_add(x_done, x_done, 1)
                                dve.reg_add(x_steps, x_steps, 3 if k == 0 else 2)
                                dve.wait_ge(x_step, dve.snap(x_steps))
                        if k == 0:
                            window_hots(it, u, 0)
                            dve.wait_ge(onehot_ready, i + 1)
                            weigh(wts[:, u % 2, :, :, :], hot[:, u % 2, :, :], cf).then_inc(wts_ready, 1)
                            window_hots(it, u, 1)
                        if k == 0 and u == 2:
                            coefficients(it + 2, (it + 1) * ST)
                        if k == 0 and u == 0:
                            dve.wait_ge(blk_summed, it + 1)
                        add_sums((u + 1) % 2, dve.snap(prev, min_val=0, max_val=N - 1), i)
                        dve.reg_mov(prev, regs[u])
                    if k == 0:
                        dve.reg_mov(blk, blk_next)
                        dve.reg_mov(blk_next, it)
                add_sums(1, dve.snap(prev, min_val=0, max_val=N - 1), GROUPS)
                dve.wait_ge(psum_free, (GROUPS + 1) * (k + 1) + 1)
                dve.nop().then_inc(sums_ready, 1)
                if k == 0:
                    for j in range(2):
                        blk_sums(STEPS + j, j, slice((NBLK - 2 + j) * P, (NBLK - 1 + j) * P), GROUPS + 2)
                    dve.wait_ge(win_read, NW + 2)
                    link(dve.tensor_reduce(faults[:, 1:2], above_sum[:, :], axis=AX, op=ALU.add))
                    link(dve.tensor_reduce(faults[:, 7:8], faults[:, 0:6], axis=AX, op=ALU.add))
                    dve.nop().then_inc(faults_in, 1)
                    last = [(STEPS + j, j, slice(NBLK - 2 + j, NBLK - 1 + j)) for j in range(2)]
                    for n in range(2):
                        for at in last:
                            blk_layer(n, *at)
                    for at in last:
                        blk_norm(*at)
                    for n in range(6):
                        for at in last:
                            blk_split(n, *at)
                    dve.wait_ge(parts_ready, STEPS + 3)

            def banks(width, p=P):
                return ps[0:p, 0:-(-NBLK // 8), :].rearrange("p k (b d) -> p (k b) d", d=D)[:, 0:NBLK, 0:width]

            def per_node(v, w):
                return v.unsqueeze(2).to_broadcast([P, NBLK, w])

            def per_feature(v, w):
                return v.unsqueeze(1).to_broadcast([P, NBLK, w])

            def transposed(n, p, into):
                for q in range(-(-NBLK // 4)):
                    w = min(4, NBLK - 4 * q) * P
                    dve.wait_ge(node_mm, n + q + 1)
                    dve.tensor_copy(into[:, q * 512:q * 512 + w], ps[0:p, q % 8, 0:w]).then_inc(ps_read, 1)

            NQ = -(-NBLK // 4)
            xb_v, g_v, xc_v = xb[:, :, :], g_rows, xc[:, 0:NBLK, :]

            def general():
                link = chain(general_step)
                dve.wait_ge(s_xb, 32)
                dve.wait_ge(node_mm, 1)
                link(dve.tensor_tensor(xc_v, banks(D), per_feature(bias_bc[:, :], D), ALU.add))
                link(dve.scalar_tensor_tensor(out=xb_v, in0=xc_v, scalar=0.0, in1=xb_v, op0=ALU.max, op1=ALU.add))
                link(norm(xb_v, centred, xc_v, P, NBLK, 2, link))
                dve.nop().then_inc(node_in, 1)
                transposed(1, D, acc[0:D, 1, 0:NBLK * P])
                dve.wait_ge(ps_read, NQ)
                dve.memset(acc[:, 0, :], 0.0)
                dve.nop().then_inc(node_in, 1)
                link(dve.memset(g_v[:, :, HID:D], 0.0))
                link(dve.memset(g_v[:, :, HID:HID + 1], 1.0))
                dve.wait_ge(node_mm, 2 + NQ)
                link(dve.tensor_copy(g_v[:, :, 0:HID], banks(HID)))
                dve.nop().then_inc(table_rows_ready, 1)
                link(dve.tensor_tensor(right1, banks(2 * HID)[:, :, HID:2 * HID], per_feature(b1_bc[:, :], HID),
                                       ALU.add))
                aggregate(1)
                dve.wait_ge(node_mm, 3 + NQ)
                link(dve.tensor_scalar(recip_cnt[:, :].unsqueeze(2), banks(HID + 1)[:, :, HID:HID + 1], 1.0, None,
                                       ALU.max))
                link(dve.reciprocal(recip_cnt[:, :], recip_cnt[:, :]))
                hid = g_v[:, :, 0:HID]
                link(dve.tensor_tensor(hid, banks(HID), per_node(recip_cnt[:, :], HID), ALU.mult))
                link(dve.tensor_tensor(hid, hid, right1, ALU.add))
                link(dve.tensor_scalar(hid, hid, 0.0, None, ALU.max))
                dve.nop().then_inc(table_rows_ready, 1)
                dve.nop().then_inc(node_in, 1)
                transposed(3 + NQ, HID, acc[0:HID, 1, 0:NBLK * P])
                dve.wait_ge(ps_read, 2 * NQ)
                link(dve.memset(acc[:, 0, :], 0.0))
                dve.nop().then_inc(node_in, 1)
                dve.wait_ge(node_mm, 4 + 2 * NQ)
                link(dve.tensor_tensor(xb_v, xb_v, banks(D), ALU.add))
                link(dve.tensor_tensor(xb_v, xb_v, per_feature(b2_bc[:, :], D), ALU.add))
                aggregate(2)
                dve.wait_ge(node_mm, 5 + 2 * NQ)
                link(dve.tensor_tensor(g_v, banks(D), per_node(recip_cnt[:, :], D), ALU.mult))
                link(dve.tensor_tensor(g_v, g_v, xb_v, ALU.add))
                dve.nop().then_inc(table_rows_ready, 1)

            CHUNK_STEPS = 11

            def hidden(c, blk0, w):
                link = chain(chunk_step, c * CHUNK_STEPS)
                sums = ps[:, 4, 0:w * D].rearrange("p (q c) -> p q c", c=D)
                hid, rest, rc = hid_c[:, 0:w, :], rest_c[:, 0:w, :], recip_cnt[:, bass.ds(blk0, w)]
                hi, mid_, lo = (parts2[:, bass.ds(blk0, w), a:a + HID] for a in (0, HID + 1, 2 * HID + 1))
                nodes = xb[:, bass.ds(blk0, w), :]
                dve.wait_ge(sums_mm, c + 1)
                link(dve.tensor_scalar(rc.unsqueeze(2), sums[:, :, HID:HID + 1], 1.0, None, ALU.max))
                dve.sem_inc(recip_begun, 1)
                link(dve.reciprocal(rc, rc))
                link(dve.tensor_tensor(hid, sums[:, :, 0:HID], rc.unsqueeze(2).to_broadcast([P, w, HID]), ALU.mult))
                link(dve.tensor_tensor(hid, hid, right1[:, bass.ds(blk0, w), :], ALU.add))
                dve.tensor_scalar(hid, hid, 0.0, None, ALU.max).then_inc(hid_ready, 1)
                dve.wait_ge(hid_ready, c + 1)
                link(dve.tensor_copy(hi, hid))
                link(dve.tensor_tensor(rest, hid, hi, ALU.subtract))
                link(dve.tensor_copy(mid_, rest))
                link(dve.tensor_tensor(rest, rest, mid_, ALU.subtract))
                link(dve.tensor_copy(lo, rest))
                dve.nop().then_inc(parts2_ready, 1)
                dve.wait_ge(root_mm, c + 1)
                link(dve.tensor_tensor(nodes, nodes, ps[:, 6, 0:w * D].rearrange("p (q c) -> p q c", c=D), ALU.add))
                link(dve.tensor_tensor(nodes, nodes, b2_bc[:, :].unsqueeze(1).to_broadcast([P, w, D]), ALU.add))

            def output(e, blk0, w):
                res = g_rows[:, bass.ds(blk0, w), :]
                dve.wait_ge(out_mm, e + 1)
                dve.tensor_tensor(res, ps[:, 4, 0:w * D].rearrange("p (q c) -> p q c", c=D),
                                  recip_cnt[:, bass.ds(blk0, w)].unsqueeze(2).to_broadcast([P, w, D]),
                                  ALU.mult).then_inc(out_step, 1)
                dve.wait_ge(out_step, e + 1)
                dve.tensor_tensor(res, res, xb[:, bass.ds(blk0, w), :], ALU.add).then_inc(out_ready, 1)

            def dense():
                dve.memset(parts2[:, :, HID:HID + 1], 1.0).then_inc(parts2_ready, 1)
                hidden(0, NBLK - 1, 1)
                with dve.Fori(0, TRIPS) as it:
                    for n in range(NBUF):
                        hidden(it * NBUF + (n + 1), it * (-NBUF * 4) + (FULLC - 1 - n) * 4, 4)
                with dve.Fori(0, TRIPS) as it:
                    for n in range(NBUF):
                        output(it * NBUF + n, it * (NBUF * 4) + n * 4, 4)
                output(FULLC, NBLK - 1, 1)

            aggregate(0)
            dve.wait_ge(faults_mm, 1)
            link(dve.tensor_scalar(faults[0:1, 6:7], ps[0:1, 2, 0:1], 1.0, None, ALU.min))
            link(dve.tensor_copy(fault_i[:, :], faults[0:1, 6:7]))
            dve.nop().then_inc(fault_known, 1)
            fault = dve.value_load(fault_i[0:1, 0:1], min_val=0, max_val=1)
            with dve.If(fault > 0):
                general()
            with dve.Else():
                dense()
            dve.nop()

        @block.tensor
        def _(pe):
            pe.sem_inc(mm_done, U)
            pe.sem_inc(early_mm, 1)
            pe.sem_inc(win_mm, 2)
            pe.wait_ge(pool_consts, POOL_CONSTS)
            pe.wait_ge(low_high_ready, 1)
            for k in range(3):
                ins = pe.transpose(ps[0:BLK, 6, k * P:(k + 1) * P], low_high[:, k, 0:BLK], ident[:, :])
            ins.then_inc(low_high_tr, 1)
            pe.wait_ge(rows_cast, 1)
            for n in range(12):
                tile = (src_rows_f, wgt_rows, dst_rows_f)[n // 4]
                if n == 4:
                    pe.wait_ge(s_wgt, 48)
                if n >= 6:
                    pe.wait_ge(cols_copied, n - 5)
                for b in range(4 * (n % 4), min(4 * (n % 4) + 4, BLK)):
                    ins = pe.transpose(ps[:, n % 6, (b % 4) * P:(b % 4 + 1) * P], tile[:, b, :], ident[:, :])
                ins.then_inc(tr_done, 1)
            pe.wait_ge(dst_copied, 4)
            pe.wait_ge(cols_copied, 8)

            def type_rows(n_expr, done_before):
                pe.wait_ge(types_hot_ready, n_expr)
                if done_before is not None:
                    pe.wait_ge(coef_done, done_before)
                for g in range(U):
                    for part in range(3):
                        ins = pe.matmul(ps[:, 5, g * TPG * NB:(g + 1) * TPG * NB],
                                        types_hot[:, g * SUB:(g + 1) * SUB], comp_parts[:, part, :],
                                        start=part == 0, stop=part == 2)
                ins.then_inc(coef_mm, 1)

            def window(it, u, j):
                pe.wait_ge(hots_ready, it * WPS + (WPS + 2 * u + j + 1))
                pe.wait_ge(win_read, it * WPS + (2 * u + j + 1))
                for v in range(WVIS):
                    ins = pe.matmul(ps[:, 3 + j, 0:WCOL], row_hot[:, j, v, :], col_hot[:, j, v, :],
                                    start=v == 0, stop=v == WVIS - 1)
                ins.then_inc(win_mm, 1)

            pe.wait_ge(comp_ready, 1)
            type_rows(1, None)
            x_seen = pe.alloc_register("pe_x_seen")
            pe.reg_mov(x_seen, 0)
            regs = [pe.alloc_register(f"pe_extra{n}") for n in range(U)]

            def products(slot, hots, weights, k, u):
                for t in range(TPG):
                    if k:
                        ins = pe.matmul(ps[0:D, slot, 0:WIN], rows[:, u, t, :], hots[:, t, :],
                                        start=t == 0, stop=t == TPG - 1)
                        continue
                    for half in range(2):
                        ins = pe.matmul(ps[half * D:(half + 1) * D, slot, 0:2 * WIN], rows[:, u, t, :],
                                        weights[:, t, 2 * half:2 * half + 2, :].rearrange("p b w -> p (b w)"),
                                        start=t == 0, stop=t == TPG - 1)
                return ins

            def blk_products(i, j):
                pe.wait_ge(blk_summed, i + 1)
                for h in range(2):
                    ins = pe.matmul(blk_banks[j][0][:, 0:D], blk_sum[:, j, h, :], basis_sb[:, h, :],
                                    start=h == 0, stop=h == 1)
                ins.then_inc(blk_mm, 1)

            def blk_transpose(i, j, read=2 * STEPS + 1):
                if j == 0:
                    pe.wait_ge(early_read, read)
                pe.wait_ge(blk_normed, i + 1)
                pe.sem_inc(pe_waited, 1)
                pe.transpose(blk_banks[j][1][0:D, 0:P], blk_rows[:, j, :], ident[:, :]).then_inc(blk_tr, 1)

            def blk_times_w1(i, j):
                pe.wait_ge(blk_t_ready, i + 1)
                pe.matmul(blk_banks[j][0][:, D:2 * D], blk_t[:, j, :], w1_sb[:, :],
                          start=True, stop=True).then_inc(blk_w1_mm, 1)

            def early_sums(n, h, second):
                if not second:
                    pe.wait_ge(early_read, n + 1)
                    pe.sem_inc(pe_waited, 1)
                for b in range(NBLK // 2, NBLK) if second else range(NBLK // 2):
                    ins = pe.matmul(early_ps, parts1[:, b, :], a_half[:, h, b, :],
                                    start=b == 0, stop=b == NBLK - 1)
                if second:
                    ins.then_inc(early_mm, 1)

            def aggregate(k):
                with pe.Fori(0, STEPS) as it:
                    pe.load(regs, meta[0:1, 1, bass.ds(it * U, U)])
                    for u in range(U):
                        i = it * U + u
                        if k == 0 and u == 0:
                            type_rows(it + 2, it + 1)
                        extra = pe.snap(regs[u], min_val=0, max_val=XMAX - 1)
                        with pe.If(extra > 0):
                            pe.wait_ge(gathered[u], it * (16 * TPG) + 16 * TPG * (STEPS * k + 1))
                            pe.sem_inc(pe_waited, 1)
                            with pe.Fori(0, extra):
                                pe.wait_ge(x_wts_ready, pe.snap(x_seen) + 1)
                                products(2, x_hot[:, :, :], x_wts[:, :, :, :], k, u).then_inc(x_mm_done, 1)
                                pe.reg_add(x_seen, x_seen, 1)
                        if k == 0:
                            window(it, u, 0)
                        pe.wait_ge(gathered[u], it * (16 * TPG) + 16 * TPG * (STEPS * k + 1))
                        pe.wait_ge(wts_ready, i + (GROUPS * k + 1))
                        pe.wait_ge(psum_free, i + ((GROUPS + 1) * k + 1))
                        products(u % 2, hot[:, u % 2, :, :], wts[:, u % 2, :, :, :], k, u).then_inc(mm_done, 1)
                        if k == 0:
                            window(it, u, 1)
                            if u == 0:
                                blk_products(it, 0)
                            if u == 3:
                                blk_transpose(it, 0, it * 2 + 2)
                            if u == 0:
                                pe.wait_ge(win_read, it * WPS + 2)
                                pe.wait_ge(parts_ready, it + 1)
                            if u == 4:
                                pe.wait_ge(win_read, it * WPS + (HW + 2))
                                pe.wait_ge(blk_t_ready, it + 1)
                            if u in (0, 1):
                                early_sums(it * 2, 1, u == 1)
                            if u in (4, 5):
                                early_sums(it * 2 + 1, 0, u == 5)
                            if u == 5:
                                blk_times_w1(it, 0)

            def from_sums(wide, rhs):
                for b in range(NBLK):
                    for h in range(len(rhs)):
                        k_rows = rhs[h].shape[0]
                        ins = pe.matmul(ps[:, b // 8, (b % 8) * D:(b % 8) * D + wide],
                                        acc[0:k_rows, h, b * P:(b + 1) * P], rhs[h],
                                        start=h == 0, stop=h == len(rhs) - 1)
                ins.then_inc(node_mm, 1)

            def transposes(tile, wide, read_before):
                for b in range(NBLK):
                    if b % 4 == 0 and b // 4 >= 8:
                        pe.wait_ge(ps_read, read_before + b // 4 - 7)
                    ins = pe.transpose(ps[0:wide, b // 4 % 8, (b % 4) * P:(b % 4 + 1) * P], tile[:, b, 0:wide],
                                       ident[:, :])
                    if b % 4 == 3 or b == NBLK - 1:
                        ins.then_inc(node_mm, 1)

            def from_transposed(p, rhs):
                for b in range(NBLK):
                    ins = pe.matmul(ps[:, b // 8, (b % 8) * D:(b % 8 + 1) * D], acc[0:p, 1, b * P:(b + 1) * P], rhs,
                                    start=True, stop=True)
                ins.then_inc(node_mm, 1)

            def dense_begins(n):
                pe.wait_ge(conv_read, n)
                pe.sem_inc(pe_waited, 1)

            def dense(buf, bank, blocks, lo, hi, parts):
                for q in range(lo, hi):
                    b, halves = blocks[q]
                    ins = pe.matmul(ps[0:H3W, bank, 0:halves * HDST], parts[:, b, :],
                                    a_buf[buf][:, 0:halves, b * HDST:(b + 1) * HDST],
                                    start=q == 0, stop=q == len(blocks) - 1)
                if hi == len(blocks):
                    ins.then_inc(conv_mm, 1)

            def times(done, stage, w, weights, wide, early=None):
                for q in range(w):
                    cols = slice(q * P, (q + 1) * P)
                    ins = pe.matmul(ps[:, 4, q * D:q * D + wide], sums_st[0:H3W, stage, cols], weights,
                                    start=True, stop=early is None)
                    if early is not None:
                        ins = pe.matmul(ps[:, 4, q * D:q * D + wide], early_ld[0:H3W, early, cols], weights,
                                        start=False, stop=True)
                ins.then_inc(done, 1)

            def sums_hidden(e):
                pe.wait_ge(conv_read, e + (NBUF + 1))
                early = e % NBUF if 0 < e < FULLC else None
                if early is not None:
                    pe.wait_ge(early_loaded[early], 16 * ((e - 1) // NBUF + 1))
                times(sums_mm, (e - 1) % NBUF if e else 0, 4 if e else 1, from_parts[:, :], HID + 1, early)

            def transpose_hidden(e):
                pe.wait_ge(hid_ready, e + 1)
                for q in range(4 if e else 1):
                    ins = pe.transpose(ps[0:HID, 5, q * P:(q + 1) * P], hid_c[:, q, :], ident[:, :])
                ins.then_inc(hid_tr, 1)

            def times_w2r(e):
                pe.wait_ge(hid_t_ready, e + 1)
                for q in range(4 if e else 1):
                    ins = pe.matmul(ps[:, 6, q * D:(q + 1) * D], hid_t[:, q * P:(q + 1) * P], w2r_sb[:, :],
                                    start=True, stop=True)
                ins.then_inc(root_mm, 1)

            def sums_out(f, stage, w):
                pe.wait_ge(conv_read, f + (NBUF + FULLC + 2))
                if not (isinstance(f, int) and f == 0):
                    pe.wait_ge(out_ready, f)
                times(out_mm, stage, w, w2l_sb[:, :], D)

            def first_pass():
                pe.wait_ge(parts_ready, STEPS + 1)
                pe.wait_ge(a_loaded[0], 16)
                dense_begins(1)
                blocks = [(b, RESTH) for b in range(NBLK)]
                dense(0, NBUF, blocks, 0, NBLK - 2, parts1)
                pe.wait_ge(parts_ready, STEPS + 3)
                dense(0, NBUF, blocks, NBLK - 2, NBLK, parts1)
                for e in range(1, FULLC + 1):
                    c = FULLC - e
                    buf, bank = e % NBUF, (e - 1) % NBUF
                    blocks = [(b, CH) for b in range(NBLK)]
                    if c:
                        full = blocks[4 * c + 2:]
                        some = [(b, 2 * (b - 4 * c) + 5) for b in range(4 * c - 2, 4 * c + 2)]
                        blocks = full[:-1] + some + full[-1:]
                    n = len(blocks)
                    pe.wait_ge(a_loaded[buf], 16 * (e // NBUF + 1))
                    dense_begins(e + 1)
                    dense(buf, bank, blocks, 0, n // 3, parts1)
                    sums_hidden(e - 1)
                    dense(buf, bank, blocks, n // 3, 2 * n // 3, parts1)
                    transpose_hidden(e - 1)
                    dense(buf, bank, blocks, 2 * n // 3, n, parts1)
                    times_w2r(e - 1)
                sums_hidden(FULLC)

            def second_trip(it, first):
                blocks = [(q, CH) for q in reversed(range(NBLK))]
                for n in range(NBUF):
                    b = BUF2[n]
                    f = it * NBUF + n
                    pe.wait_ge(a_loaded[b], it * 16 + 16 * (FULLC // NBUF + (b == 0)))
                    dense_begins(it * NBUF + (FULLC + 2 + n))
                    if first and n == 0:
                        dense(b, n, blocks, 0, 12, parts2)
                        transpose_hidden(FULLC)
                        dense(b, n, blocks, 12, 24, parts2)
                        times_w2r(FULLC)
                        dense(b, n, blocks, 24, NBLK - 4, parts2)
                        pe.wait_ge(parts2_ready, FULLC + 2)
                        dense(b, n, blocks, NBLK - 4, NBLK, parts2)
                    else:
                        dense(b, n, blocks, 0, 20, parts2)
                        sums_out(f + -1, (n - 1) % NBUF, 4)
                        dense(b, n, blocks, 20, NBLK, parts2)

            def sage_dense():
                first_pass()
                pe.wait_ge(parts2_ready, FULLC + 1)
                second_trip(0, True)
                with pe.Fori(1, TRIPS) as it:
                    second_trip(it, False)
                pe.wait_ge(a_loaded[0], 16 * (2 * TRIPS + 1))
                dense_begins(2 * FULLC + 2)
                blocks = [(b, RESTH) for b in range(NBLK)]
                dense(0, NBUF, blocks, 0, 20, parts2)
                sums_out(FULLC - 1, NBUF - 1, 4)
                dense(0, NBUF, blocks, 20, NBLK, parts2)
                sums_out(FULLC, 0, 1)

            NQ = -(-NBLK // 4)
            pe.wait_ge(meta_back, 32)
            pe.wait_ge(s_consts, CONST_DMAS)
            aggregate(0)
            for stage in (blk_products, blk_transpose, blk_times_w1):
                for j in range(2):
                    stage(STEPS + j, j)
                if stage is blk_products:
                    pe.wait_ge(faults_in, 1)
                    pe.matmul(ps[0:1, 2, 0:1], faults[:, 7:8], ones[:, :], start=True, stop=True).then_inc(faults_mm, 1)
            pe.wait_ge(fault_known, 1)
            fault = pe.value_load(fault_i[0:1, 0:1], min_val=0, max_val=1)

            def general():
                pe.wait_ge(sums_ready, 1)
                from_sums(D, [basis_sb[:, 0, :], basis_sb[:, 1, :]])
                pe.wait_ge(node_in, 1)
                transposes(xc, D, 0)
                pe.wait_ge(node_in, 2)
                from_transposed(D, w1_sb[:, :])
                aggregate(1)
                pe.wait_ge(sums_ready, 2)
                from_sums(HID + 1, [from_parts[0:D, :]])
                pe.wait_ge(node_in, 3)
                transposes(g_rows, HID, NQ)
                pe.wait_ge(node_in, 4)
                from_transposed(HID, w2r_sb[:, :])
                aggregate(2)
                pe.wait_ge(sums_ready, 3)
                from_sums(D, [w2l_sb[0:D, :]])

            with pe.If(fault > 0):
                general()
            with pe.Else():
                sage_dense()
            pe.nop()


_INS = ['x', 'src', 'dst', 'edge_type_32', 'edge_weight', 'L0_gnn_weight', 'L0_gnn_w_comp', 'L0_gnn_bias',
        'L1_gnn_W1_l', 'L1_gnn_b1', 'L1_gnn_W1_r', 'L1_gnn_W2_l', 'L1_gnn_b2', 'L1_gnn_W2_r']


def kernel(**inputs):
    import numpy as _np
    import concourse.bacc as _bacc
    from concourse import mybir as _mybir
    from concourse.bass_utils import run_bass_kernel_spmd as _run

    nc = _bacc.Bacc("TRN2", target_bir_lowering=False, num_devices=1)
    arrays, args = {}, []
    for name in _INS:
        a = _np.ascontiguousarray(inputs[name])
        arrays[f"in_{name}"] = a
        args.append(nc.dram_tensor(f"in_{name}", a.shape, _mybir.dt.from_np(a.dtype), kind="ExternalInput").ap())
    args.append(nc.dram_tensor("out_0", tuple(inputs['x'].shape), _mybir.dt.float32, kind="ExternalOutput").ap())
    gnn_kernel(nc, *args)
    r = _run(nc, [arrays], core_ids=[0])
    return r.results[0]["out_0"]
```
